# Optimizing a Trainium2 kernel written in Bass

```python
import numpy as np
import jax
import jax.numpy as jnp

def _softmax(x, axis=-1):
    return jax.nn.softmax(x, axis=axis)

def _gelu(x):
    return jax.nn.gelu(x, approximate=True)

def _silu(x):
    return jax.nn.silu(x)

def _sigmoid(x):
    return jax.nn.sigmoid(x)

def _layernorm(x, axis=-1, eps=1e-05):
    m = jnp.mean(x, axis=axis, keepdims=True)
    v = jnp.var(x, axis=axis, keepdims=True)
    return (x - m) / jnp.sqrt(v + eps)

def _scatter_add(tgt, idx, src, axis=0):
    return tgt.at[idx].add(src)

def _segment_sum(src, seg, n):
    return jax.ops.segment_sum(src, seg, n)
kernel_name = 'mk_flamingo_gated_d1_seqx_r8_572e47'

def setup_inputs(seed: int=0):
    np.random.seed(seed)
    _w = jnp.asarray

    def _rec_inputs():
        import jax
        import jax.numpy as jnp
        _rk = jax.random.key(seed)
        x = 7.22e-05 + 1 * jax.random.normal(jax.random.fold_in(_rk, 1), (8, 256, 128), jnp.float32)
        _lenS = 256 - jax.random.randint(jax.random.fold_in(_rk, 7), (8,), 0, max(1, 256 // 4) + 1, jnp.int32)
        _lenS2 = 256 - jax.random.randint(jax.random.fold_in(_rk, 8), (8,), 0, max(1, 256 // 4) + 1, jnp.int32)
        _ctx_1024P = jax.random.normal(jax.random.fold_in(_rk, 11), (8, 16, 128), jnp.float32)
        _ctx_1024c = jax.random.dirichlet(jax.random.fold_in(_rk, 511), 0.3 * jnp.ones((16,), jnp.float32), (8, 256))
        _ctx_1024t = jnp.einsum('bsk,bkd->bsd', _ctx_1024c, _ctx_1024P)
        _ctx_1024t = _ctx_1024t * jax.lax.rsqrt(jnp.mean(jnp.square(_ctx_1024t)) + 1e-12) * 0.953939
        ctx_1024 = 4.13588e-05 + 0.999923 * (_ctx_1024t + 0.3 * jax.random.normal(jax.random.fold_in(_rk, 611), (8, 256, 128), jnp.float32))
        _g = jax.random.normal(jax.random.fold_in(_rk, 9001), (2, 1), jnp.float32)
        _g = jnp.sign(_g) * jnp.maximum(jnp.abs(_g), 1.0) + (_g == 0) * 1.0
        g_xattn = _g[0]
        g_ffn = _g[1]
        return (x, ctx_1024, g_xattn, g_ffn)
    x, ctx_1024, g_xattn, g_ffn = _rec_inputs()

    def _L0_xattn_setup():
        import jax, jax.numpy as jnp
        import numpy as np
        B, S, D = (4, 256, 128)
        key = jax.random.key(seed)
        ks = jax.random.split(key, 10)
        sc = 1.0 / np.sqrt(D)
        return {'x': jax.random.normal(ks[0], (B, S, D), dtype=jnp.float32), 'y': jax.random.normal(ks[1], (B, S, D), dtype=jnp.float32), 'Wq': jax.random.normal(ks[2], (D, D), dtype=jnp.float32) * sc, 'bq': jnp.zeros((D,), dtype=jnp.float32), 'Wk': jax.random.normal(ks[3], (D, D), dtype=jnp.float32) * sc, 'bk': jnp.zeros((D,), dtype=jnp.float32), 'Wv': jax.random.normal(ks[4], (D, D), dtype=jnp.float32) * sc, 'bv': jnp.zeros((D,), dtype=jnp.float32), 'Wr': jax.random.normal(ks[5], (D, D), dtype=jnp.float32) * sc, 'br': jnp.zeros((D,), dtype=jnp.float32)}
    _L0_xattn_all = _L0_xattn_setup()
    _L0_xattn_in = {k: v for k, v in _L0_xattn_all.items() if k in ('Wq', 'bq', 'Wk', 'bk', 'Wv', 'bv', 'Wr', 'br')}
    del _L0_xattn_all

    def _L0_ffn_setup():
        import jax, jax.numpy as jnp
        import numpy as np
        E = 8
        TOP_K = 2
        B, S, D = (2, 512, 128)
        H = 512
        CAPACITY = 256

        def _moe(x, Wg, W1, b1, W2, b2):
            b, s, d = x.shape
            xf = x.reshape(b * s, d)
            logits = xf.astype(jnp.float32) @ Wg.astype(jnp.float32)
            probs = jax.nn.softmax(logits, axis=-1)
            vals, idx = jax.lax.top_k(probs, TOP_K)
            w = vals / (jnp.sum(vals, axis=-1, keepdims=True) + 1e-09)
            counts = jnp.zeros((E,), dtype=jnp.int32)
            combine = jnp.zeros((b * s, E), dtype=jnp.float32)
            for k in range(TOP_K):
                oh = jax.nn.one_hot(idx[:, k], E, dtype=jnp.int32)
                pos = jnp.cumsum(oh, axis=0) - 1 + counts[None, :]
                keep = (oh == 1) & (pos < CAPACITY)
                counts = counts + jnp.sum(keep.astype(jnp.int32), axis=0)
                combine = combine + w[:, k][:, None] * keep.astype(jnp.float32)
            out = jnp.zeros_like(xf)
            for e in range(E):
                h = jax.nn.gelu(xf @ W1[e] + b1[e])
                ye = h @ W2[e] + b2[e]
                out = out + combine[:, e][:, None].astype(xf.dtype) * ye
            return out.reshape(b, s, d)
        key = jax.random.key(seed)
        k0, k1, k2, k3 = jax.random.split(key, 4)
        return {'x': jax.random.normal(k0, (B, S, D), dtype=jnp.float32), 'Wg': jax.random.normal(k1, (D, E), dtype=jnp.float32) * 0.02, 'W1': jax.random.normal(k2, (E, D, H), dtype=jnp.float32) * 0.02, 'b1': jnp.zeros((E, H), dtype=jnp.float32), 'W2': jax.random.normal(k3, (E, H, D), dtype=jnp.float32) * 0.02, 'b2': jnp.zeros((E, D), dtype=jnp.float32)}
    _L0_ffn_all = _L0_ffn_setup()
    _L0_ffn_in = {k: v for k, v in _L0_ffn_all.items() if k in ('Wg', 'W1', 'b1', 'W2', 'b2')}
    del _L0_ffn_all
    return {'x': x, 'ctx_1024': ctx_1024, 'g_xattn': g_xattn, 'g_ffn': g_ffn, 'L0_xattn_Wq': _L0_xattn_in['Wq'], 'L0_xattn_bq': _L0_xattn_in['bq'], 'L0_xattn_Wk': _L0_xattn_in['Wk'], 'L0_xattn_bk': _L0_xattn_in['bk'], 'L0_xattn_Wv': _L0_xattn_in['Wv'], 'L0_xattn_bv': _L0_xattn_in['bv'], 'L0_xattn_Wr': _L0_xattn_in['Wr'], 'L0_xattn_br': _L0_xattn_in['br'], 'L0_ffn_Wg': _L0_ffn_in['Wg'], 'L0_ffn_W1': _L0_ffn_in['W1'], 'L0_ffn_b1': _L0_ffn_in['b1'], 'L0_ffn_W2': _L0_ffn_in['W2'], 'L0_ffn_b2': _L0_ffn_in['b2']}

def reference(x, ctx_1024, g_xattn, g_ffn, L0_xattn_Wq, L0_xattn_bq, L0_xattn_Wk, L0_xattn_bk, L0_xattn_Wv, L0_xattn_bv, L0_xattn_Wr, L0_xattn_br, L0_ffn_Wg, L0_ffn_W1, L0_ffn_b1, L0_ffn_W2, L0_ffn_b2):
    import jax
    import jax.numpy as jnp

    def _L0_xattn_ref(x, y, Wq, bq, Wk, bk, Wv, bv, Wr, br):
        import jax, jax.numpy as jnp
        import numpy as np
        B, S, D = (4, 256, 128)
        Q = jnp.einsum('bsd,de->bse', x, Wq) + bq
        K = jnp.einsum('bsd,de->bse', y, Wk) + bk
        V = jnp.einsum('bsd,de->bse', y, Wv) + bv
        K_hat = jnp.cos(jnp.einsum('bsd,dr->bsr', K, Wr) + br)
        scores = jnp.einsum('bqr,bkr->bqk', Q, K_hat)
        probs = jax.nn.softmax(scores, axis=-1)
        return jnp.einsum('bqk,bkd->bqd', probs, V)

    def _L0_ffn_ref(x, Wg, W1, b1, W2, b2):
        import jax, jax.numpy as jnp
        import numpy as np
        E = 8
        TOP_K = 2
        B, S, D = (2, 512, 128)
        H = 512
        CAPACITY = 256

        def _moe(x, Wg, W1, b1, W2, b2):
            b, s, d = x.shape
            xf = x.reshape(b * s, d)
            logits = xf.astype(jnp.float32) @ Wg.astype(jnp.float32)
            probs = jax.nn.softmax(logits, axis=-1)
            vals, idx = jax.lax.top_k(probs, TOP_K)
            w = vals / (jnp.sum(vals, axis=-1, keepdims=True) + 1e-09)
            counts = jnp.zeros((E,), dtype=jnp.int32)
            combine = jnp.zeros((b * s, E), dtype=jnp.float32)
            for k in range(TOP_K):
                oh = jax.nn.one_hot(idx[:, k], E, dtype=jnp.int32)
                pos = jnp.cumsum(oh, axis=0) - 1 + counts[None, :]
                keep = (oh == 1) & (pos < CAPACITY)
                counts = counts + jnp.sum(keep.astype(jnp.int32), axis=0)
                combine = combine + w[:, k][:, None] * keep.astype(jnp.float32)
            out = jnp.zeros_like(xf)
            for e in range(E):
                h = jax.nn.gelu(xf @ W1[e] + b1[e])
                ye = h @ W2[e] + b2[e]
                out = out + combine[:, e][:, None].astype(xf.dtype) * ye
            return out.reshape(b, s, d)
        return _moe(x, Wg, W1, b1, W2, b2)
    x = x + jnp.tanh(g_xattn[0]) * _L0_xattn_ref(_layernorm(x, axis=-1), ctx_1024, L0_xattn_Wq, L0_xattn_bq, L0_xattn_Wk, L0_xattn_bk, L0_xattn_Wv, L0_xattn_bv, L0_xattn_Wr, L0_xattn_br)
    x = x + jnp.tanh(g_ffn[0]) * _L0_ffn_ref(_layernorm(x, axis=-1), L0_ffn_Wg, L0_ffn_W1, L0_ffn_b1, L0_ffn_W2, L0_ffn_b2)
    return x

_drawn_inputs = setup_inputs


def setup_inputs(seed=0):
    import zlib

    import numpy as np

    out = dict(_drawn_inputs(seed))
    spreads = {'L0_xattn_bq': (0.0, 0.1),
     'L0_xattn_bk': (0.0, 0.1),
     'L0_xattn_bv': (0.0, 0.1),
     'L0_xattn_br': (0.0, 0.1),
     'L0_ffn_b1': (0.0, 0.8),
     'L0_ffn_b2': (0.0, 0.1)}
    factors = {'L0_ffn_W1': 2.681}
    for name, (base, spread) in spreads.items():
        noise = np.random.default_rng([zlib.crc32(name.encode()), seed]).standard_normal(out[name].shape)
        drawn = base * np.exp(spread * noise) if base else spread * noise
        out[name] = jnp.asarray(drawn.astype(out[name].dtype))
    for name, factor in factors.items():
        out[name] = (out[name] * factor).astype(out[name].dtype)
    return out
```

```python
from contextlib import ExitStack

import numpy as np
import concourse.bass as bass
from concourse import mybir

F32 = mybir.dt.float32
F16 = mybir.dt.float16
I32 = mybir.dt.int32
U32 = mybir.dt.uint32
ALU = mybir.AluOpType
ACT = mybir.ActivationFunctionType
AX = mybir.AxisListType

P = 128
CAPACITY = 256
TOP_K = 2
LN_EPS = 1e-5
WEIGHT_EPS = 1e-9
TWO_PI = 6.283185307179586
SIN_SCALE = 6.283185
ROUND_MAGIC = 12582912.0


def build(nc, x, ctx_in, g_xattn, g_ffn, Wq, bq, Wk, bk, Wv, bv, Wr, br, Wg, W1, b1, W2, b2, out, x2_rows):
    B, S, D = x.shape
    E, _, H = W1.shape
    N = B * S
    T = N // P
    TB = S // P
    GT = 4
    G = T // GT
    GB = GT // TB
    C = H // P
    SLOT_TILES = E * CAPACITY // P
    ST = CAPACITY // P
    ROW = D + E
    PAD = CAPACITY
    assert D == P and TB == 2 and ST == 2 and N <= 2048

    x_rows = x.rearrange("b s d -> (b s) d")
    c_rows = ctx_in.rearrange("b s d -> (b s) d")

    ctx = ExitStack()
    with ctx:
        def sb(name, shape, dt=F32):
            return ctx.enter_context(nc.sbuf_tensor(name, shape, dt))

        def sem(name):
            return ctx.enter_context(nc.semaphore(name))

        bank = [ctx.enter_context(nc.psum_tensor(f"bank{i}", [P, 512], F32)) for i in range(8)]

        ident = sb("ident", [P, P])
        tri = sb("tri", [P, P], F16)
        ones = sb("ones", [P, P], F16)
        lane_iota = sb("lane_iota", [P, P], F16)
        tile_iota = sb("tile_iota", [P, SLOT_TILES], F16)
        expert_iota = sb("expert_iota", [P, E], F16)
        token_no = sb("token_no", [P, T])
        pad_row = sb("pad_row", [P, SLOT_TILES])
        neg_half = sb("neg_half", [P, 8])
        neg_one = sb("neg_one", [P, 8])
        zeros = sb("zeros", [P, 2 * ROW])
        wk = sb("wk", [P, P])
        wr = sb("wr", [P, P])
        wv = sb("wv", [P, P])
        wq = sb("wq", [P, P])
        wg = sb("wg", [P, E])
        bias_rows = sb("bias_rows", [E * C + 3, P])
        bias_cols = sb("bias_cols", [P, E * C + 3])
        BQ, BK, BR = E * C, E * C + 1, E * C + 2
        bv_all = sb("bv_all", [P, D])
        b2_all = sb("b2_all", [P, E, D])
        gates = sb("gates", [P, 2])
        tgates = sb("tgates", [P, 2])
        gated_bv = sb("gated_bv", [P, D])
        wkT = sb("wkT", [P, P])
        wkr = sb("wkr", [P, P])
        turn0 = sb("turn0", [P, 1])
        turn = sb("turn", [P, 1])
        w1 = sb("w1", [P, E, H])
        w2 = sb("w2", [P, E, C, D])
        y_in = sb("y_in", [P, T, D])
        x_in = sb("x_in", [P, T, D])
        yT = sb("yT", [P, T, P])
        stats1 = sb("stats1", [P, T, 6])
        mv1 = sb("mv1", [P, T, 2])
        rstd1 = sb("rstd1", [P, T])
        xn = sb("xn", [P, 2, GT, D])
        xnT = sb("xnT", [P, 2, GT * P])
        qT = sb("qT", [P, N])
        turns = sb("turns", [P, 2, GT * P])
        whole = sb("whole", [P, 2, GT * P])
        frac = sb("frac", [P, 2, GT * P])
        khatT = sb("khatT", [P, N])
        v = sb("v", [P, T, D])
        neg_max = sb("neg_max", [P, B, TB])
        den = sb("den", [P, B, TB])
        rden = sb("rden", [P, B, TB])
        alpha = sb("alpha", [P, B, TB])
        probs = sb("probs", [P, 2, TB, S])
        probsT = sb("probsT", [P, 2, TB, S])
        x1 = sb("x1", [P, T, D])
        stats2 = sb("stats2", [P, T, 6])
        mv2 = sb("mv2", [P, T, 2])
        rstd2 = sb("rstd2", [P, T])
        rows = sb("rows", [P, T, ROW])
        x2T = sb("x2T", [P, 2, TB * P])
        top = sb("top", [P, T, 8])
        top_at = sb("top_at", [P, T, 8], U32)
        top_diff = sb("top_diff", [P, T, 8])
        top_exp = sb("top_exp", [P, T, 8])
        exp_sum = sb("exp_sum", [P, T])
        w_den = sb("w_den", [P, T])
        w_top = sb("w_top", [P, T, TOP_K])
        onehot = sb("onehot", [P, T, TOP_K, E], F16)
        before = sb("before", [P, T + 1, TOP_K * E], F16)
        comb0 = sb("comb0", [P, T, E])
        comb1 = sb("comb1", [P, T, E])
        picked = sb("picked", [P, T * TOP_K, E])
        pos = sb("pos", [P, T * TOP_K])
        kept1 = sb("kept1", [P, E])
        picked1 = sb("picked1", [P, T, E])
        shift1 = sb("shift1", [P, T])
        upper = sb("upper", [P, T * TOP_K])
        over = sb("over", [P, T * TOP_K])
        lane = sb("lane", [P, T * TOP_K])
        slot_tile = sb("slot_tile", [P, T * TOP_K])
        lane_hot = sb("lane_hot", [P, T * TOP_K, P], F16)
        tile_hot = sb("tile_hot", [P, T * TOP_K, SLOT_TILES], F16)
        gather_at = sb("gather_at", [P, SLOT_TILES], I32)
        scatter_at = sb("scatter_at", [P, SLOT_TILES], I32)
        empty = sb("empty", [P, SLOT_TILES])
        empty_row = sb("empty_row", [P, SLOT_TILES])
        xe = sb("xe", [P, SLOT_TILES, ROW])
        xeT = sb("xeT", [P, 2, CAPACITY])
        hid = sb("hid", [P, 2, C, CAPACITY])
        yb = sb("yb", [P, 2, ST, D])
        ys = sb("ys", [P, 2, ST, D])

        y_loaded = [sem(f"y_loaded{g}") for g in range(G)]
        x_loaded = [sem(f"x_loaded{g}") for g in range(G)]
        wkr_loaded = sem("wkr_loaded")
        bias_loaded = sem("bias_loaded")
        wv_loaded = sem("wv_loaded")
        wq_loaded = sem("wq_loaded")
        wg_loaded = sem("wg_loaded")
        gates_loaded = sem("gates_loaded")
        bv_loaded = sem("bv_loaded")
        b2_loaded = sem("b2_loaded")
        w1_loaded = [sem(f"w1_loaded{i}") for i in range(4)]
        w2_loaded = [sem(f"w2_loaded{i}") for i in range(4)]
        pool_step = sem("pool_step")
        consts_ready = sem("consts_ready")
        zeros_ready = sem("zeros_ready")
        wkT_ready, bias_psum, bias_ready, wkT_copied = sem("wkT_ready"), sem("bias_psum"), sem("bias_ready"), sem("wkT_copied")
        wkr_psum, wkr_ready, turn_psum, turn0_ready, turn_ready = (sem("wkr_psum"), sem("wkr_ready"), sem("turn_psum"),
                                                                   sem("turn0_ready"), sem("turn_ready"))
        yT_psum, yT_ready = sem("yT_psum"), sem("yT_ready")
        xT_psum, xT_ready = sem("xT_psum"), sem("xT_ready")
        stats1_ready, mv1_ready, var1_ready, rstd1_ready, xn_ready = (sem("stats1_ready"), sem("mv1_ready"),
                                                                      sem("var1_ready"), sem("rstd1_ready"), sem("xn_ready"))
        z_psum, turns_ready, whole_ready, frac_ready, khat_ready = (sem("z_psum"), sem("turns_ready"), sem("whole_ready"),
                                                                    sem("frac_ready"), sem("khat_ready"))
        v_psum, v_ready, q_psum, q_ready = sem("v_psum"), sem("v_ready"), sem("q_psum"), sem("q_ready")
        tanh_ready, gated_bv_ready, xb_ready = sem("tanh_ready"), sem("gated_bv_ready"), sem("xb_ready")
        scores_psum, max_ready, probs_ready = sem("scores_psum"), sem("max_ready"), sem("probs_ready")
        probsT_psum, probsT_ready, pv_psum = sem("probsT_psum"), sem("probsT_ready"), sem("pv_psum")
        rden_ready, alpha_ready, x1_ready = sem("rden_ready"), sem("alpha_ready"), sem("x1_ready")
        stats2_ready, mv2_ready, var2_ready, rstd2_ready, x2_ready = (sem("stats2_ready"), sem("mv2_ready"),
                                                                      sem("var2_ready"), sem("rstd2_ready"), sem("x2_ready"))
        x2T_psum, x2T_ready, logits_psum = sem("x2T_psum"), sem("x2T_ready"), sem("logits_psum")
        top_ready, top_at_ready, onehot_ready, before_ready = (sem("top_ready"), sem("top_at_ready"), sem("onehot_ready"),
                                                               sem("before_ready"))
        diff_ready, exp_ready, exp_sum_ready = sem("diff_ready"), sem("exp_ready"), sem("exp_sum_ready")
        weight_step, comb1_ready, comb_ready = sem("weight_step"), sem("comb1_ready"), sem("comb_ready")
        x1_stored, rows_stored, pads_stored = sem("x1_stored"), sem("rows_stored"), sem("pads_stored")
        cum_psum, route_step = sem("cum_psum"), sem("route_step")
        lane_hot_ready, table_psum = sem("lane_hot_ready"), sem("table_psum")
        gather_at_ready, scatter_at_ready = sem("gather_at_ready"), sem("scatter_at_ready")
        gathered = [sem(f"gathered{e}") for e in range(E)]
        xeT_psum, xeT_ready, up_psum, hid_ready = sem("xeT_psum"), sem("xeT_ready"), sem("up_psum"), sem("hid_ready")
        down_psum, yb_ready, ys_ready, scattered = sem("down_psum"), sem("yb_ready"), sem("ys_ready"), sem("scattered")

        yT_bank = [bank[0], bank[1]]
        z_bank = [bank[2], bank[3]]
        v_bank = [bank[4], bank[5]]
        xT_bank, q_bank = bank[6], bank[7]
        scores_bank = [bank[0], bank[1]]
        probsT_bank = [bank[2], bank[3]]
        pv_bank, x2T_bank, logits_bank = bank[4], bank[5], bank[6]
        cum_bank, table_bank = bank[7], bank[5]
        up_bank = [bank[0:2], bank[2:4]]
        xeT_bank = [bank[4], bank[6]]
        down_bank = [bank[5], bank[7]]
        logits_ps = logits_bank[:, 0:TB * E].rearrange("p (h e) -> p h e", h=TB)
        cum_ps = cum_bank[:, 0:T * TOP_K * E]
        kept_ps = cum_bank[:, T * TOP_K * E:T * TOP_K * E + E]
        table_ps = table_bank[:, 0:SLOT_TILES]

        block = ctx.enter_context(nc.Block())

        @block.sync
        def _(sp):
            def load_rows(dst, src, g, signal):
                sp.dma_start(dst[:, g * GT:(g + 1) * GT, :],
                             src[g * GT * P:(g + 1) * GT * P, :].rearrange("(t p) d -> p t d", p=P)).then_inc(signal[g], 16)

            def store_rows(b):
                sp.wait_ge(comb_ready, b + 1)
                sp.wait_ge(x2_ready, (b + 1) * TB)
                sp.dma_start(x2_rows[1 + b * S:1 + (b + 1) * S, :].rearrange("(t p) d -> p t d", p=P),
                             rows[:, b * TB:(b + 1) * TB, :]).then_inc(rows_stored, 16)

            load_rows(y_in, c_rows, 0, y_loaded)
            load_rows(x_in, x_rows, 0, x_loaded)
            for g in range(1, G):
                load_rows(y_in, c_rows, g, y_loaded)
                load_rows(x_in, x_rows, g, x_loaded)
            sp.dma_start(b2_all[:, :, :], b2.rearrange("e d -> (e d)").partition_broadcast(P)
                         .rearrange("p (e d) -> p e d", e=E)).then_inc(b2_loaded, 16)
            for i in range(4):
                es = slice(i * E // 4, (i + 1) * E // 4)
                sp.dma_start(w1[:, es, :], W1[es].rearrange("e d h -> d e h")).then_inc(w1_loaded[i], 16)
                for e in range(i * E // 4, (i + 1) * E // 4):
                    sp.dma_start(w2[:, e, :, :], W2[e].rearrange("(c p) d -> p c d", p=P)).then_inc(w2_loaded[i], 16)
            sp.wait_ge(zeros_ready, 1)
            sp.dma_start(x2_rows[0:1, :], zeros[0:1, 0:ROW]).then_inc(pads_stored, 16)
            sp.dma_start(out[0:PAD, :].rearrange("(t p) d -> p t d", p=P),
                         zeros[:, 0:PAD // P * D].rearrange("p (t d) -> p t d", d=D)).then_inc(pads_stored, 16)
            for b in range(B):
                ts = slice(b * TB, (b + 1) * TB)
                sp.wait_ge(x1_ready, b + 1)
                sp.dma_start(out[PAD + b * S:PAD + (b + 1) * S, :].rearrange("(t p) d -> p t d", p=P),
                             x1[:, ts, :]).then_inc(x1_stored, 16)
                if b >= 1:
                    store_rows(b - 1)
            store_rows(B - 1)
            sp.wait_ge(x1_stored, 16 * B)
            sp.wait_ge(pads_stored, 32)
            sp.wait_ge(scattered, 16 * SLOT_TILES)

        @block.gpsimd
        def _(pool):
            pool.memset(ident[:, :], 0.0).then_inc(pool_step, 1)
            pool.memset(tri[:, :], 1.0).then_inc(pool_step, 1)
            pool.memset(ones[:, :], 1.0).then_inc(consts_ready, 1)
            pool.memset(neg_half[:, :], -0.5).then_inc(consts_ready, 1)
            pool.memset(neg_one[:, :], -1.0).then_inc(consts_ready, 1)
            pool.wait_ge(pool_step, 2)
            pool.affine_select(out=ident[:, :], in_=ident[:, :], compare_op=ALU.not_equal, fill=1.0, base=0,
                               pattern=[[-1, P]], channel_multiplier=1).then_inc(consts_ready, 1)
            pool.affine_select(out=tri[:, :], in_=tri[:, :], compare_op=ALU.is_ge, fill=0.0, base=0,
                               pattern=[[1, P]], channel_multiplier=-1).then_inc(consts_ready, 1)
            pool.memset(before[:, 0, :], 0.0).then_inc(consts_ready, 1)
            small = dict(allow_small_or_imprecise_dtypes=True)
            pool.iota(lane_iota[:, :], [[1, P]], base=1, channel_multiplier=0, **small).then_inc(consts_ready, 1)
            pool.iota(tile_iota[:, :], [[1, SLOT_TILES]], base=0, channel_multiplier=0, **small).then_inc(consts_ready, 1)
            pool.iota(expert_iota[:, :], [[1, E]], base=0, channel_multiplier=0, **small).then_inc(consts_ready, 1)
            pool.iota(token_no[:, :], [[P, T]], base=1, channel_multiplier=1, **small).then_inc(consts_ready, 1)
            pool.iota(pad_row[:, :].rearrange("p (e s) -> p e s", s=ST), [[0, E], [P, ST]], base=-(PAD - 1),
                      channel_multiplier=1, **small).then_inc(consts_ready, 1)
            pool.memset(zeros[:, :], 0.0).then_inc(zeros_ready, 1)

            def inv_std(mv, rstd, t0, n, var_sem, rstd_sem, k):
                pool.tensor_scalar(rstd[:, t0:t0 + n], mv[:, t0:t0 + n, 1], LN_EPS, None, ALU.add).then_inc(var_sem, 1)
                pool.wait_ge(var_sem, k)
                pool.tensor_tensor(rstd[:, t0:t0 + n], rstd[:, t0:t0 + n], neg_half[:, 0:n], ALU.pow).then_inc(rstd_sem, 1)
                pool.wait_ge(rstd_sem, k)

            def norm1(g):
                pool.wait_ge(mv1_ready, g + 1)
                inv_std(mv1, rstd1, g * GT, GT, var1_ready, rstd1_ready, g + 1)
                if g >= 2:
                    pool.wait_ge(xT_psum, g - 1)
                for i in range(GT):
                    t = g * GT + i
                    last = pool.tensor_scalar(xn[:, g % 2, i, :], x_in[:, t, :], mv1[:, t, 0:1], rstd1[:, t:t + 1],
                                              ALU.subtract, ALU.mult)
                last.then_inc(xn_ready, 1)

            def fraction(g):
                pool.wait_ge(turns_ready, g + 1)
                if g >= 2:
                    pool.wait_ge(khat_ready, g - 1)
                pool.tensor_scalar(whole[:, g % 2, :], turns[:, g % 2, :], ROUND_MAGIC, ROUND_MAGIC,
                                   ALU.add, ALU.subtract).then_inc(whole_ready, 1)
                pool.wait_ge(whole_ready, g + 1)
                pool.tensor_tensor(frac[:, g % 2, :], turns[:, g % 2, :], whole[:, g % 2, :],
                                   ALU.subtract).then_inc(frac_ready, 1)

            def add_bv(g):
                pool.wait_ge(xn_ready, g + 1)
                ts = slice(g * GT, (g + 1) * GT)
                pool.tensor_tensor(x_in[:, ts, :], x_in[:, ts, :],
                                   gated_bv[:, :].unsqueeze(1).broadcast_to([P, GT, D]), ALU.add).then_inc(xb_ready, 1)

            norm1(0)
            norm1(1)
            fraction(0)
            norm1(2)
            fraction(1)
            norm1(3)
            fraction(2)
            fraction(3)
            pool.wait_ge(tanh_ready, 1)
            pool.wait_ge(bv_loaded, 16)
            pool.tensor_scalar(gated_bv[:, :], bv_all[:, :], tgates[:, 0:1], None, ALU.mult).then_inc(gated_bv_ready, 1)
            pool.wait_ge(gated_bv_ready, 1)
            add_bv(0)

            def norm2(b):
                pool.wait_ge(mv2_ready, b + 1)
                inv_std(mv2, rstd2, b * TB, TB, var2_ready, rstd2_ready, b + 1)
                for t in range(b * TB, (b + 1) * TB):
                    pool.tensor_scalar(rows[:, t, 0:D], x1[:, t, :], mv2[:, t, 0:1], rstd2[:, t:t + 1],
                                       ALU.subtract, ALU.mult).then_inc(x2_ready, 1)

            def gaps(b):
                ts = slice(b * TB, (b + 1) * TB)
                pool.wait_ge(top_ready, b + 1)
                pool.tensor_tensor(top_diff[:, ts, :], top[:, ts, :], top[:, ts, 0:1].broadcast_to([P, TB, 8]),
                                   ALU.subtract).then_inc(diff_ready, 1)
                pool.wait_ge(onehot_ready, b + 1)
                for t in range(b * TB, (b + 1) * TB):
                    if t:
                        pool.wait_ge(before_ready, t)
                    pool.tensor_tensor(before[:, t + 1, :], before[:, t, :],
                                       onehot[:, t, :, :].rearrange("p k e -> p (k e)"), ALU.add).then_inc(before_ready, 1)

            def weights(b):
                ts = slice(b * TB, (b + 1) * TB)
                pool.wait_ge(exp_sum_ready, b + 1)
                k = 5 * b
                pool.tensor_scalar(w_den[:, ts], exp_sum[:, ts], WEIGHT_EPS, 1.0, ALU.mult, ALU.add).then_inc(weight_step, 1)
                pool.wait_ge(weight_step, k + 1)
                pool.tensor_tensor(w_den[:, ts], w_den[:, ts], top_exp[:, ts, 1], ALU.add).then_inc(weight_step, 1)
                pool.wait_ge(weight_step, k + 2)
                pool.tensor_tensor(w_den[:, ts], w_den[:, ts], neg_one[:, 0:TB], ALU.pow).then_inc(weight_step, 1)
                pool.wait_ge(weight_step, k + 3)
                pool.tensor_scalar(w_top[:, ts, 0], w_den[:, ts], tgates[:, 1:2], None, ALU.mult).then_inc(weight_step, 1)
                pool.wait_ge(weight_step, k + 4)
                pool.tensor_tensor(w_top[:, ts, 1], w_top[:, ts, 0], top_exp[:, ts, 1], ALU.mult)
                pool.tensor_tensor(comb0[:, ts, :], onehot[:, ts, 0, :], w_top[:, ts, 0:1].broadcast_to([P, TB, E]),
                                   ALU.mult).then_inc(weight_step, 1)
                pool.wait_ge(weight_step, k + 5)
                pool.tensor_tensor(comb1[:, ts, :], onehot[:, ts, 1, :], w_top[:, ts, 1:2].broadcast_to([P, TB, E]),
                                   ALU.mult).then_inc(comb1_ready, 1)
                pool.wait_ge(comb1_ready, b + 1)
                pool.tensor_tensor(rows[:, ts, D:ROW], comb0[:, ts, :], comb1[:, ts, :], ALU.add).then_inc(comb_ready, 1)

            for s in range(B + 4):
                if 1 <= s <= B:
                    norm2(s - 1)
                if s + 1 < G:
                    add_bv(s + 1)
                if 3 <= s < B + 3:
                    gaps(s - 3)
                if 4 <= s:
                    weights(s - 4)

            def gather(j):
                pool.indirect_dma_start(out=xe[:, j, :], out_offset=None, in_=x2_rows[:, :],
                                        in_offset=bass.IndirectOffsetOnAxis(ap=gather_at[:, j:j + 1], axis=0))\
                    .then_inc(gathered[j // ST], 16)

            AHEAD = 3 * ST
            pool.wait_ge(rows_stored, 16 * B)
            pool.wait_ge(pads_stored, 32)
            pool.wait_ge(gather_at_ready, 1)
            for j in range(AHEAD):
                gather(j)
            pool.wait_ge(scatter_at_ready, 1)
            pool.wait_ge(x1_stored, 16 * B)
            for e in range(E):
                pool.wait_ge(ys_ready, e + 1)
                if e:
                    pool.wait_ge(scattered, 16 * ST * e)
                for j in range(e * ST, (e + 1) * ST):
                    pool.indirect_dma_start(out=out[:, :],
                                            out_offset=bass.IndirectOffsetOnAxis(ap=scatter_at[:, j:j + 1], axis=0),
                                            in_=ys[:, e % 2, j % ST, :], in_offset=None,
                                            compute_op=ALU.add).then_inc(scattered, 16)
                for j in range(e * ST + AHEAD, min((e + 1) * ST + AHEAD, SLOT_TILES)):
                    gather(j)

        @block.scalar
        def _(act):
            act.dma_start(wk[:, :], Wk).then_inc(wkr_loaded, 16)
            act.dma_start(wr[:, :], Wr).then_inc(wkr_loaded, 16)
            act.dma_start(bias_rows[0:E * C, :], b1.rearrange("e (c p) -> (e c) p", p=P)).then_inc(bias_loaded, 16)
            for at, vec in ((BQ, bq), (BK, bk), (BR, br)):
                act.dma_start(bias_rows[at:at + 1, :], vec.rearrange("(a p) -> a p", a=1)).then_inc(bias_loaded, 16)
            act.dma_start(wv[:, :], Wv).then_inc(wv_loaded, 16)
            act.dma_start(wq[:, :], Wq).then_inc(wq_loaded, 16)
            act.dma_start(gates[:, 0:1], g_xattn.partition_broadcast(P)).then_inc(gates_loaded, 16)
            act.dma_start(gates[:, 1:2], g_ffn.partition_broadcast(P)).then_inc(gates_loaded, 16)
            act.dma_start(bv_all[:, :], bv.partition_broadcast(P)).then_inc(bv_loaded, 16)
            act.dma_start(wg[:, :], Wg).then_inc(wg_loaded, 16)

            def copy_yT(g):
                act.wait_ge(yT_psum, g + 1)
                act.activation(yT[:, g * GT:(g + 1) * GT, :].rearrange("p t c -> p (t c)"), yT_bank[g % 2][:, :],
                               ACT.Copy).then_inc(yT_ready, 1)

            def copy_xT(g):
                act.wait_ge(xT_psum, g + 1)
                if g >= 2:
                    act.wait_ge(q_psum, g - 1)
                act.activation(xnT[:, g % 2, :], xT_bank[:, :], ACT.Copy).then_inc(xT_ready, 1)

            def copy_v(g):
                act.wait_ge(v_psum, g + 1)
                act.activation(v[:, g * GT:(g + 1) * GT, :].rearrange("p t d -> p (t d)"), v_bank[g % 2][:, :],
                               ACT.Copy).then_inc(v_ready, 1)

            def cosine(g):
                act.wait_ge(frac_ready, g + 1)
                act.activation(khatT[:, g * GT * P:(g + 1) * GT * P], frac[:, g % 2, :], ACT.Sin,
                               scale=SIN_SCALE).then_inc(khat_ready, 1)

            copy_yT(0)
            copy_yT(1)
            copy_xT(0)
            copy_v(0)
            copy_yT(2)
            cosine(0)
            copy_v(1)
            copy_xT(1)
            copy_yT(3)
            cosine(1)
            copy_v(2)
            copy_xT(2)
            cosine(2)
            copy_v(3)
            copy_xT(3)
            cosine(3)
            act.wait_ge(gates_loaded, 32)
            act.activation(tgates[:, :], gates[:, :], ACT.Tanh).then_inc(tanh_ready, 1)

            for s in range(B + 4):
                if 1 <= s <= B:
                    b = s - 1
                    act.wait_ge(probsT_psum, b + 1)
                    if b >= 2:
                        act.wait_ge(pv_psum, b - 1)
                    act.activation(probsT[:, b % 2, :, :].rearrange("p h q -> p (h q)"), probsT_bank[b % 2][:, :],
                                   ACT.Copy).then_inc(probsT_ready, 1)
                if 3 <= s < B + 3:
                    b = s - 3
                    act.wait_ge(x2T_psum, b + 1)
                    if b >= 2:
                        act.wait_ge(logits_psum, b - 1)
                    act.activation(x2T[:, b % 2, :], x2T_bank[:, 0:TB * P], ACT.Copy).then_inc(x2T_ready, 1)
                if s < B:
                    act.wait_ge(max_ready, s + 1)
                    if s >= 2:
                        act.wait_ge(probsT_psum, s - 1)
                    for h in range(TB):
                        act.activation(probs[:, s % 2, h, :], scores_bank[s % 2][:, h * S:(h + 1) * S], ACT.Exp,
                                       bias=neg_max[:, s, h:h + 1], accum_out=den[:, s, h:h + 1]).then_inc(probs_ready, 1)
                if 4 <= s:
                    b = s - 4
                    ts = slice(b * TB, (b + 1) * TB)
                    act.wait_ge(diff_ready, b + 1)
                    act.activation(top_exp[:, ts, :], top_diff[:, ts, :], ACT.Exp).then_inc(exp_ready, 1)

            for e in range(E):
                if e >= 2:
                    act.wait_ge(down_psum, e - 1)
                for c in range(C):
                    act.wait_ge(up_psum, e * (C // 2) + c // 2 + 1)
                    last = act.activation(hid[:, e % 2, c, :],
                                          up_bank[e % 2][c // 2][:, c % 2 * CAPACITY:(c % 2 + 1) * CAPACITY],
                                          ACT.Gelu_apprx_tanh, bias=bias_cols[:, e * C + c:e * C + c + 1])
                    if c % 2:
                        last.then_inc(hid_ready, 1)

        @block.tensor
        def _(pe):
            pe.wait_ge(consts_ready, 11)

            def turn_y(g):
                pe.wait_ge(y_loaded[g], 16)
                if g >= 2:
                    pe.wait_ge(yT_ready, g - 1)
                for i in range(GT):
                    last = pe.transpose(yT_bank[g % 2][:, i * P:(i + 1) * P], y_in[:, g * GT + i, :], ident[:, :])
                last.then_inc(yT_psum, 1)

            def turn_x(g):
                pe.wait_ge(xn_ready, g + 1)
                if g:
                    pe.wait_ge(xT_ready, g)
                for i in range(GT):
                    last = pe.transpose(xT_bank[:, i * P:(i + 1) * P], xn[:, g % 2, i, :], ident[:, :])
                last.then_inc(xT_psum, 1)

            def keys(g):
                pe.wait_ge(yT_ready, g + 1)
                pe.wait_ge(wkr_ready, 1)
                if g >= 2:
                    pe.wait_ge(turns_ready, g - 1)
                pe.matmul(z_bank[g % 2][:, :], wkr[:, :], yT[:, g * GT:(g + 1) * GT, :].rearrange("p t c -> p (t c)"),
                          start=True, stop=True).then_inc(z_psum, 1)
                pe.wait_ge(wv_loaded, 16)
                if g >= 2:
                    pe.wait_ge(v_ready, g - 1)
                for i in range(GT):
                    last = pe.matmul(v_bank[g % 2][:, i * D:(i + 1) * D], yT[:, g * GT + i, :], wv[:, :],
                                     start=True, stop=True)
                last.then_inc(v_psum, 1)

            def queries(g):
                pe.wait_ge(xT_ready, g + 1)
                if g:
                    pe.wait_ge(q_ready, g)
                else:
                    pe.wait_ge(wq_loaded, 16)
                    pe.wait_ge(turn0_ready, 1)
                pe.matmul(q_bank[:, :], wq[:, :], xnT[:, g % 2, :], start=True, stop=True).then_inc(q_psum, 1)

            pe.wait_ge(wkr_loaded, 32)
            pe.transpose(xT_bank[:, 0:P], wk[:, :], ident[:, :]).then_inc(wkT_ready, 1)
            pe.wait_ge(bias_loaded, 64)
            pe.transpose(q_bank[:, 0:E * C + 3], bias_rows[:, :], ident[0:E * C + 3, 0:E * C + 3]).then_inc(bias_psum, 1)
            turn_y(0)
            pe.wait_ge(wkT_copied, 1)
            pe.matmul(xT_bank[:, 0:P], wkT[:, :], wr[:, :], start=True, stop=True).then_inc(wkr_psum, 1)
            pe.wait_ge(bias_ready, 1)
            pe.matmul(q_bank[:, 0:1], wr[:, :], bias_cols[:, BK:BK + 1], start=True, stop=True).then_inc(turn_psum, 1)
            turn_y(1)
            keys(0)
            turn_x(0)
            turn_y(2)
            keys(1)
            queries(0)
            turn_x(1)
            turn_y(3)
            keys(2)
            queries(1)
            turn_x(2)
            keys(3)
            queries(2)
            turn_x(3)
            queries(3)

            for s in range(B + 3):
                if s < B:
                    g = s // GB
                    pe.wait_ge(khat_ready, g + 1)
                    pe.wait_ge(q_ready, g + 1)
                    if s >= 2:
                        pe.wait_ge(probs_ready, TB * (s - 1))
                    for h in range(TB):
                        q0 = s * S + h * P
                        last = pe.matmul(scores_bank[s % 2][:, h * S:(h + 1) * S], qT[:, q0:q0 + P],
                                         khatT[:, s * S:(s + 1) * S], start=True, stop=True)
                    last.then_inc(scores_psum, 1)
                if 1 <= s <= B:
                    b = s - 1
                    pe.wait_ge(probs_ready, TB * (b + 1))
                    if b >= 2:
                        pe.wait_ge(probsT_ready, b - 1)
                    for k in range(TB):
                        for h in range(TB):
                            c0 = k * S + h * P
                            last = pe.transpose(probsT_bank[b % 2][:, c0:c0 + P], probs[:, b % 2, h, k * P:(k + 1) * P],
                                                ident[:, :])
                    last.then_inc(probsT_psum, 1)
                if 3 <= s:
                    b = s - 3
                    pe.wait_ge(x2_ready, TB * (b + 1))
                    if b:
                        pe.wait_ge(x2T_ready, b)
                    for h in range(TB):
                        last = pe.transpose(x2T_bank[:, h * P:(h + 1) * P], rows[:, b * TB + h, 0:D], ident[:, :])
                    last.then_inc(x2T_psum, 1)
                if 1 <= s <= B:
                    b = s - 1
                    pe.wait_ge(probsT_ready, b + 1)
                    pe.wait_ge(v_ready, b // GB + 1)
                    if b:
                        pe.wait_ge(x1_ready, b)
                    for h in range(TB):
                        for k in range(TB):
                            last = pe.matmul(pv_bank[:, h * D:(h + 1) * D], probsT[:, b % 2, k, h * P:(h + 1) * P],
                                             v[:, b * TB + k, :], start=(k == 0), stop=(k == TB - 1))
                    last.then_inc(pv_psum, 1)
                if 3 <= s:
                    b = s - 3
                    pe.wait_ge(x2T_ready, b + 1)
                    if b:
                        pe.wait_ge(top_at_ready, b)
                    else:
                        pe.wait_ge(wg_loaded, 16)
                    for h in range(TB):
                        last = pe.matmul(logits_ps[:, h, :], x2T[:, b % 2, h * P:(h + 1) * P], wg[:, :],
                                         start=True, stop=True)
                    last.then_inc(logits_psum, 1)

            pe.wait_ge(before_ready, T)
            pe.matmul(cum_ps, tri[:, :], onehot[:, :, :, :].rearrange("p t k e -> p (t k e)"), start=True, stop=False)
            pe.matmul(cum_ps, ones[:, :], before[:, 0:T, :].rearrange("p t c -> p (t c)"), start=False, stop=True)
            pe.matmul(kept_ps, ones[:, :], before[:, T, 0:E], start=True, stop=True).then_inc(cum_psum, 1)
            for n in range(T * TOP_K):
                pe.wait_ge(lane_hot_ready, n + 1)
                last = pe.matmul(table_ps, lane_hot[:, n, :], tile_hot[:, n, :], start=(n == 0), stop=(n == T * TOP_K - 1))
            last.then_inc(table_psum, 1)

            def turn_xe(e):
                pe.wait_ge(gathered[e], 16 * ST)
                if e >= 2:
                    pe.wait_ge(xeT_ready, e - 1)
                for h in range(ST):
                    last = pe.transpose(xeT_bank[e % 2][:, h * P:(h + 1) * P], xe[:, e * ST + h, 0:D], ident[:, :])
                last.then_inc(xeT_psum, 1)

            def up(e):
                if e % 2 == 0:
                    pe.wait_ge(w1_loaded[e // 2], 16)
                pe.wait_ge(xeT_ready, e + 1)
                for c in range(C):
                    if e >= 2 and c % 2 == 0:
                        pe.wait_ge(hid_ready, (e - 2) * (C // 2) + c // 2 + 1)
                    last = pe.matmul(up_bank[e % 2][c // 2][:, c % 2 * CAPACITY:(c % 2 + 1) * CAPACITY],
                                     w1[:, e, c * P:(c + 1) * P], xeT[:, e % 2, :], start=True, stop=True)
                    if c % 2:
                        last.then_inc(up_psum, 1)

            def down(e):
                if e % 2 == 0:
                    pe.wait_ge(w2_loaded[e // 2], 32)
                pe.wait_ge(hid_ready, (e + 1) * (C // 2))
                if e >= 2:
                    pe.wait_ge(yb_ready, e - 1)
                else:
                    pe.wait_ge(scatter_at_ready, 1)
                for h in range(ST):
                    for c in range(C):
                        last = pe.matmul(down_bank[e % 2][:, h * D:(h + 1) * D], hid[:, e % 2, c, h * P:(h + 1) * P],
                                         w2[:, e, c, :], start=(c == 0), stop=(c == C - 1))
                last.then_inc(down_psum, 1)

            turn_xe(0)
            for e in range(E + 1):
                if e + 1 < E:
                    turn_xe(e + 1)
                if e < E:
                    up(e)
                if e:
                    down(e - 1)

        @block.vector
        def _(dve):
            def stats(src, st, mv, t0, n, st_sem, mv_sem, k):
                for t in range(t0, t0 + n):
                    last = dve.bn_stats(st[:, t, :], src[:, t, :])
                last.then_inc(st_sem, 1)
                dve.wait_ge(st_sem, k)
                for t in range(t0, t0 + n):
                    last = dve.bn_aggr(mv[:, t, :], st[:, t, :])
                last.then_inc(mv_sem, 1)

            def stats_x(g):
                dve.wait_ge(x_loaded[g], 16)
                stats(x_in, stats1, mv1, g * GT, GT, stats1_ready, mv1_ready, g + 1)

            def copy_turns(g):
                dve.wait_ge(z_psum, g + 1)
                if g >= 2:
                    dve.wait_ge(frac_ready, g - 1)
                dve.tensor_scalar(turns[:, g % 2, :], z_bank[g % 2][:, :], turn[:, 0:1], None, ALU.add)\
                    .then_inc(turns_ready, 1)

            def copy_q(g):
                dve.wait_ge(q_psum, g + 1)
                dve.tensor_scalar(qT[:, g * GT * P:(g + 1) * GT * P], q_bank[:, :], bias_cols[:, BQ:BQ + 1], None,
                                  ALU.add).then_inc(q_ready, 1)

            dve.wait_ge(wkT_ready, 1)
            dve.tensor_copy(wkT[:, :], xT_bank[:, 0:P]).then_inc(wkT_copied, 1)
            dve.wait_ge(bias_psum, 1)
            dve.tensor_copy(bias_cols[:, :], q_bank[:, 0:E * C + 3]).then_inc(bias_ready, 1)
            stats_x(0)
            dve.wait_ge(wkr_psum, 1)
            dve.tensor_scalar(wkr[:, :], xT_bank[:, 0:P], 1.0 / TWO_PI, None, ALU.mult).then_inc(wkr_ready, 1)
            dve.wait_ge(turn_psum, 1)
            dve.wait_ge(bias_ready, 1)
            dve.tensor_scalar(turn0[:, :], q_bank[:, 0:1], bias_cols[:, BR:BR + 1], None, ALU.add).then_inc(turn0_ready, 1)
            dve.wait_ge(turn0_ready, 1)
            dve.tensor_scalar(turn[:, :], turn0[:, :], 1.0 / TWO_PI, 0.25, ALU.mult, ALU.add).then_inc(turn_ready, 1)
            stats_x(1)
            dve.wait_ge(turn_ready, 1)
            copy_turns(0)
            stats_x(2)
            copy_turns(1)
            copy_q(0)
            stats_x(3)
            copy_turns(2)
            copy_q(1)
            copy_turns(3)
            copy_q(2)
            copy_q(3)

            def scores_max(b):
                dve.wait_ge(scores_psum, b + 1)
                dve.tensor_reduce(neg_max[:, b, :], scores_bank[b % 2][:, :].rearrange("p (h k) -> p h k", h=TB), AX.X,
                                  ALU.max, negate=True).then_inc(max_ready, 1)

            def residual(b):
                dve.wait_ge(probs_ready, TB * (b + 1))
                dve.reciprocal(rden[:, b, :], den[:, b, :]).then_inc(rden_ready, 1)
                if b == 0:
                    dve.wait_ge(tanh_ready, 1)
                dve.wait_ge(rden_ready, b + 1)
                dve.tensor_scalar(alpha[:, b, :], rden[:, b, :], tgates[:, 0:1], None, ALU.mult).then_inc(alpha_ready, 1)
                dve.wait_ge(alpha_ready, b + 1)
                dve.wait_ge(xb_ready, b // GB + 1)
                dve.wait_ge(pv_psum, b + 1)
                for h in range(TB):
                    t = b * TB + h
                    last = dve.scalar_tensor_tensor(out=x1[:, t, :], in0=pv_bank[:, h * D:(h + 1) * D],
                                                    scalar=alpha[:, b, h:h + 1], in1=x_in[:, t, :],
                                                    op0=ALU.mult, op1=ALU.add)
                last.then_inc(x1_ready, 1)
                dve.wait_ge(x1_ready, b + 1)
                stats(x1, stats2, mv2, b * TB, TB, stats2_ready, mv2_ready, b + 1)

            def route(b):
                ts = slice(b * TB, (b + 1) * TB)
                dve.wait_ge(logits_psum, b + 1)
                for h in range(TB):
                    last = dve.max(top[:, b * TB + h, :], logits_ps[:, h, :])
                last.then_inc(top_ready, 1)
                dve.wait_ge(top_ready, b + 1)
                for h in range(TB):
                    last = dve.max_index(top_at[:, b * TB + h, :], top[:, b * TB + h, :], logits_ps[:, h, :])
                last.then_inc(top_at_ready, 1)
                dve.wait_ge(top_at_ready, b + 1)
                dve.tensor_tensor(onehot[:, ts, :, :],
                                  expert_iota[:, :].unsqueeze(1).unsqueeze(1).broadcast_to([P, TB, TOP_K, E]),
                                  top_at[:, ts, 0:TOP_K].unsqueeze(3).broadcast_to([P, TB, TOP_K, E]),
                                  ALU.is_equal).then_inc(onehot_ready, 1)

            def exp_total(b):
                ts = slice(b * TB, (b + 1) * TB)
                dve.wait_ge(exp_ready, b + 1)
                dve.tensor_reduce(exp_sum[:, ts], top_exp[:, ts, :], AX.X, ALU.add).then_inc(exp_sum_ready, 1)

            dve.wait_ge(consts_ready, 11)
            for s in range(B + 4):
                if s < B:
                    scores_max(s)
                if 1 <= s <= B:
                    residual(s - 1)
                if 3 <= s < B + 3:
                    route(s - 3)
                if 4 <= s:
                    exp_total(s - 4)

            step = 0

            def chain(last):
                nonlocal step
                step += 1
                last.then_inc(route_step, 1)
                return step

            pairs = lambda a: a[:, :].rearrange("p (t k) -> p t k", k=TOP_K)
            dve.wait_ge(cum_psum, 1)
            dve.wait_ge(onehot_ready, B)
            n_picked = chain(dve.tensor_tensor(picked[:, :, :], onehot[:, :, :, :].rearrange("p t k e -> p (t k) e"),
                                               cum_ps.rearrange("p (n e) -> p n e", e=E), ALU.mult))
            n_kept = chain(dve.tensor_scalar(kept1[:, :], kept_ps, float(CAPACITY), None, ALU.min))
            dve.wait_ge(route_step, n_picked)
            n_pos = chain(dve.tensor_reduce(pos[:, :], picked[:, :, :], AX.X, ALU.add))
            dve.wait_ge(route_step, n_kept)
            n_picked1 = chain(dve.tensor_tensor(picked1[:, :, :], onehot[:, :, 1, :],
                                                kept1[:, :].unsqueeze(1).broadcast_to([P, T, E]), ALU.mult))
            dve.wait_ge(route_step, n_picked1)
            n_shift = chain(dve.tensor_reduce(shift1[:, :], picked1[:, :, :], AX.X, ALU.add))
            dve.wait_ge(route_step, n_shift)
            n_pos = chain(dve.tensor_tensor(pairs(pos)[:, :, 1], pairs(pos)[:, :, 1], shift1[:, :], ALU.add))
            dve.wait_ge(route_step, n_pos)
            n_upper = chain(dve.tensor_scalar(upper[:, :], pos[:, :], float(P), None, ALU.is_gt))
            n_over = chain(dve.tensor_scalar(over[:, :], pos[:, :], float(CAPACITY), float(SLOT_TILES), ALU.is_gt, ALU.mult))
            dve.wait_ge(route_step, n_upper)
            n_lane = chain(dve.scalar_tensor_tensor(out=lane[:, :], in0=upper[:, :], scalar=-float(P), in1=pos[:, :],
                                                    op0=ALU.mult, op1=ALU.add))
            dve.wait_ge(route_step, n_over)
            n_up = chain(dve.tensor_tensor(upper[:, :], upper[:, :], over[:, :], ALU.add))
            dve.wait_ge(route_step, n_up)
            n_tile = chain(dve.scalar_tensor_tensor(out=pairs(slot_tile), in0=top_at[:, :, 0:TOP_K], scalar=float(ST),
                                                    in1=pairs(upper), op0=ALU.mult, op1=ALU.add))
            dve.wait_ge(route_step, n_tile)
            chain(dve.tensor_tensor(tile_hot[:, :, :],
                                    tile_iota[:, :].unsqueeze(1).broadcast_to([P, T * TOP_K, SLOT_TILES]),
                                    slot_tile[:, :].unsqueeze(2).broadcast_to([P, T * TOP_K, SLOT_TILES]), ALU.is_equal))
            for n in range(T * TOP_K):
                dve.tensor_scalar(lane_hot[:, n, :], lane_iota[:, :], lane[:, n:n + 1],
                                  token_no[:, n // TOP_K:n // TOP_K + 1], ALU.is_equal, ALU.mult).then_inc(lane_hot_ready, 1)
            dve.wait_ge(table_psum, 1)
            dve.tensor_copy(gather_at[:, :], table_ps).then_inc(gather_at_ready, 1)
            n_empty = chain(dve.tensor_scalar(empty[:, :], table_ps, 0.0, None, ALU.is_equal))
            dve.wait_ge(route_step, n_empty)
            n_row = chain(dve.tensor_tensor(empty_row[:, :], empty[:, :], pad_row[:, :], ALU.mult))
            dve.wait_ge(route_step, n_row)
            dve.scalar_tensor_tensor(out=scatter_at[:, :], in0=table_ps, scalar=float(PAD - 1), in1=empty_row[:, :],
                                     op0=ALU.add, op1=ALU.add).then_inc(scatter_at_ready, 1)

            def copy_xeT(e):
                dve.wait_ge(xeT_psum, e + 1)
                if e >= 2:
                    dve.wait_ge(up_psum, (e - 1) * (C // 2))
                dve.tensor_copy(xeT[:, e % 2, :], xeT_bank[e % 2][:, 0:CAPACITY]).then_inc(xeT_ready, 1)

            copy_xeT(0)
            for e in range(E):
                if e + 1 < E:
                    copy_xeT(e + 1)
                dve.wait_ge(down_psum, e + 1)
                if e == 0:
                    dve.wait_ge(b2_loaded, 16)
                dve.tensor_tensor(yb[:, e % 2, :, :], down_bank[e % 2][:, 0:ST * D].rearrange("p (s d) -> p s d", s=ST),
                                  b2_all[:, e, :].unsqueeze(1).broadcast_to([P, ST, D]), ALU.add).then_inc(yb_ready, 1)
                dve.wait_ge(yb_ready, e + 1)
                if e >= 2:
                    dve.wait_ge(scattered, 16 * ST * (e - 1))
                for h in range(ST):
                    last = dve.tensor_scalar(ys[:, e % 2, h, :], yb[:, e % 2, h, :], xe[:, e * ST + h, D + e:D + e + 1],
                                             None, ALU.mult)
                last.then_inc(ys_ready, 1)


_INS = ['x', 'ctx_1024', 'g_xattn', 'g_ffn', 'L0_xattn_Wq', 'L0_xattn_bq', 'L0_xattn_Wk', 'L0_xattn_bk', 'L0_xattn_Wv',
        'L0_xattn_bv', 'L0_xattn_Wr', 'L0_xattn_br', 'L0_ffn_Wg', 'L0_ffn_W1', 'L0_ffn_b1', 'L0_ffn_W2', 'L0_ffn_b2']


def kernel(**inputs):
    import concourse.bacc as _bacc
    from concourse.bass_utils import run_bass_kernel_spmd as _run

    nc = _bacc.Bacc("TRN2", target_bir_lowering=False, num_devices=1)
    arrays, args = {}, []
    for name in _INS:
        a = np.ascontiguousarray(inputs[name])
        arrays[f"in_{name}"] = a
        args.append(nc.dram_tensor(f"in_{name}", a.shape, mybir.dt.from_np(a.dtype), kind="ExternalInput").ap())
    B, S, D = inputs["x"].shape
    E = inputs["L0_ffn_W1"].shape[0]
    out = nc.dram_tensor("out", (CAPACITY + B * S, D), F32, kind="ExternalOutput").ap()
    x2_rows = nc.dram_tensor("x2_rows", (1 + B * S, D + E), F32, kind="Internal").ap()
    build(nc, *args, out, x2_rows)
    r = _run(nc, [arrays], core_ids=[0])
    return r.results[0]["out"][CAPACITY:].reshape(B, S, D)
```

```python
from contextlib import ExitStack

import numpy as np
import concourse.bass as bass
from concourse import mybir

F32 = mybir.dt.float32
F16 = mybir.dt.float16
I32 = mybir.dt.int32
U32 = mybir.dt.uint32
ALU = mybir.AluOpType
ACT = mybir.ActivationFunctionType
AX = mybir.AxisListType

P = 128
CAPACITY = 256
TOP_K = 2
LN_EPS = 1e-5
WEIGHT_EPS = 1e-9
TWO_PI = 6.283185307179586
SIN_SCALE = 6.283185
ROUND_MAGIC = 12582912.0


def build(nc, x, ctxT, gates_in, key_pack, proj_pack, bv, W1, W2, b2, out, x2_rows):
    B, S, D = x.shape
    E, _, H = W1.shape
    N = B * S
    T = N // P
    TB = S // P
    GT = 4
    G = T // GT
    GB = GT // TB
    C = H // P
    SLOT_TILES = E * CAPACITY // P
    ST = CAPACITY // P
    ROW = D + E
    QUAD = 4
    QUADS = T * TOP_K // QUAD
    CONSTS = 10
    ROUTE_GROUPS = ((0, 3), (3, 6), (6, 7), (7, 8))
    PAD = CAPACITY
    assert D == P and TB == 2 and ST == 2 and N <= 2048

    x_rows = x.rearrange("b s d -> (b s) d")

    ctx = ExitStack()
    with ctx:
        def sb(name, shape, dt=F32):
            return ctx.enter_context(nc.sbuf_tensor(name, shape, dt))

        def sem(name):
            return ctx.enter_context(nc.semaphore(name))

        bank = [ctx.enter_context(nc.psum_tensor(f"bank{i}", [P, 512], F32)) for i in range(8)]

        ident = sb("ident", [P, P])
        tri = sb("tri", [P, P], F16)
        ones = sb("ones", [P, P], F16)
        lane_iota = sb("lane_iota", [P, P, QUAD], F16)
        tile_iota = sb("tile_iota", [P, SLOT_TILES, QUAD], F16)
        expert_iota = sb("expert_iota", [P, E], F16)
        token_no = sb("token_no", [P, T, TOP_K], F16)
        pad_row = sb("pad_row", [P, SLOT_TILES])
        neg_half = sb("neg_half", [P, 8])
        zeros = sb("zeros", [P, 2 * ROW])
        BQ, BK, BR = E * C, E * C + 1, E * C + 2
        keys_in = sb("keys_in", [P, 2 * P + BR + 1])
        wkT, wr, bias_cols = keys_in[:, 0:P], keys_in[:, P:2 * P], keys_in[:, 2 * P:]
        projs_in = sb("projs_in", [P, 2 * P + E])
        wv, wq, wg = projs_in[:, 0:P], projs_in[:, P:2 * P], projs_in[:, 2 * P:]
        bv_all = sb("bv_all", [P, D])
        b2_all = sb("b2_all", [P, E, D])
        gates = sb("gates", [P, 2])
        tgates = sb("tgates", [P, 2])
        gated_bv = sb("gated_bv", [P, D])
        wkr = sb("wkr", [P, P])
        turn0 = sb("turn0", [P, 1])
        turn = sb("turn", [P, 1])
        w1 = sb("w1", [P, E, H])
        w2 = sb("w2", [P, E, C, D])
        x_in = sb("x_in", [P, T, D])
        yT = sb("yT", [P, N])
        stats1 = sb("stats1", [P, T, 6])
        mv1 = sb("mv1", [P, T, 2])
        rstd1 = sb("rstd1", [P, T])
        xn = sb("xn", [P, 2, GT, D])
        xnT = sb("xnT", [P, 2, GT * P])
        qT = sb("qT", [P, N])
        turns = sb("turns", [P, 2, GT * P])
        whole = sb("whole", [P, 2, GT * P])
        frac = sb("frac", [P, 2, GT * P])
        khatT = sb("khatT", [P, N])
        v = sb("v", [P, T, D])
        neg_max = sb("neg_max", [P, B, TB])
        den = sb("den", [P, B, TB])
        rden = sb("rden", [P, B, TB])
        centred = sb("centred", [P, TB, D])
        probs = sb("probs", [P, 2, TB, S])
        probsT = sb("probsT", [P, 2, TB, S])
        x1 = sb("x1", [P, T, D])
        stats2 = sb("stats2", [P, T, 6])
        mv2 = sb("mv2", [P, T, 2])
        rstd2 = sb("rstd2", [P, T])
        rows = sb("rows", [P, T, ROW])
        x2T = sb("x2T", [P, 2, TB * P])
        top = sb("top", [P, T, 8])
        top_at = sb("top_at", [P, T, 8], U32)
        top_diff = sb("top_diff", [P, T, 8])
        top_exp = sb("top_exp", [P, T, 8])
        exp_sum = sb("exp_sum", [P, T])
        w_den = sb("w_den", [P, T])
        w_top = sb("w_top", [P, T, TOP_K])
        onehot = sb("onehot", [P, T, TOP_K, E], F16)
        before = sb("before", [P, T + 1, TOP_K * E], F16)
        comb0 = sb("comb0", [P, T, E])
        comb1 = sb("comb1", [P, T, E])
        picked = sb("picked", [P, T * TOP_K, E])
        pos = sb("pos", [P, T * TOP_K])
        kept1 = sb("kept1", [P, E])
        picked1 = sb("picked1", [P, T, E])
        shift1 = sb("shift1", [P, T])
        upper = sb("upper", [P, T * TOP_K])
        over = sb("over", [P, T * TOP_K])
        lane = sb("lane", [P, T * TOP_K], F16)
        slot_tile = sb("slot_tile", [P, T * TOP_K], F16)
        lane_hot = sb("lane_hot", [P, QUADS, P, QUAD], F16)
        tile_hot = sb("tile_hot", [P, QUADS, SLOT_TILES, QUAD], F16)
        token_hot = sb("token_hot", [P, QUADS, SLOT_TILES, QUAD], F16)
        gather_at = sb("gather_at", [P, SLOT_TILES], I32)
        scatter_at = sb("scatter_at", [P, SLOT_TILES], I32)
        empty = sb("empty", [P, SLOT_TILES])
        empty_row = sb("empty_row", [P, SLOT_TILES])
        xe = sb("xe", [P, SLOT_TILES, ROW])
        xeT = sb("xeT", [P, 2, CAPACITY])
        hid = sb("hid", [P, 2, C, CAPACITY])
        yb = sb("yb", [P, 2, ST, D])
        ys = sb("ys", [P, 2, ST, D])

        y_loaded = [sem(f"y_loaded{g}") for g in range(G)]
        x_loaded = [sem(f"x_loaded{g}") for g in range(G)]
        keys_loaded, projs_loaded = sem("keys_loaded"), sem("projs_loaded")
        gates_loaded = sem("gates_loaded")
        bv_loaded = sem("bv_loaded")
        b2_loaded = sem("b2_loaded")
        w1_loaded = [sem(f"w1_loaded{i}") for i in range(4)]
        w2_loaded = [sem(f"w2_loaded{i}") for i in range(4)]
        pool_step = sem("pool_step")
        consts_ready = sem("consts_ready")
        zeros_ready = sem("zeros_ready")
        wkr_psum, wkr_ready, turn_psum, turn0_ready, turn_ready = (sem("wkr_psum"), sem("wkr_ready"), sem("turn_psum"),
                                                                   sem("turn0_ready"), sem("turn_ready"))
        xT_psum, xT_ready = sem("xT_psum"), sem("xT_ready")
        stats1_ready, mv1_ready, var1_ready, rstd1_ready, xn_ready = (sem("stats1_ready"), sem("mv1_ready"),
                                                                      sem("var1_ready"), sem("rstd1_ready"), sem("xn_ready"))
        z_psum, turns_ready, whole_ready, frac_ready, khat_ready = (sem("z_psum"), sem("turns_ready"), sem("whole_ready"),
                                                                    sem("frac_ready"), sem("khat_ready"))
        v_psum, v_ready, q_psum, q_ready = sem("v_psum"), sem("v_ready"), sem("q_psum"), sem("q_ready")
        tanh_ready, gated_bv_ready, xb_ready = sem("tanh_ready"), sem("gated_bv_ready"), sem("xb_ready")
        scores_psum, max_ready, probs_ready = sem("scores_psum"), sem("max_ready"), sem("probs_ready")
        probsT_psum, probsT_ready, pv_psum = sem("probsT_psum"), sem("probsT_ready"), sem("pv_psum")
        rden_ready, centred_ready, x1_ready = sem("rden_ready"), sem("centred_ready"), sem("x1_ready")
        stats2_ready, mv2_ready, var2_ready, rstd2_ready, x2_ready = (sem("stats2_ready"), sem("mv2_ready"),
                                                                      sem("var2_ready"), sem("rstd2_ready"), sem("x2_ready"))
        x2T_psum, x2T_ready, logits_psum = sem("x2T_psum"), sem("x2T_ready"), sem("logits_psum")
        top_ready, top_at_ready, onehot_ready, before_ready = (sem("top_ready"), sem("top_at_ready"), sem("onehot_ready"),
                                                               sem("before_ready"))
        diff_ready, exp_ready, exp_sum_ready = sem("diff_ready"), sem("exp_ready"), sem("exp_sum_ready")
        w_den_ready, w_rec_ready, weight_step, comb_ready = (sem("w_den_ready"), sem("w_rec_ready"), sem("weight_step"),
                                                             sem("comb_ready"))
        x1_stored, rows_stored, pads_stored = sem("x1_stored"), sem("rows_stored"), sem("pads_stored")
        cum_psum, route_step = sem("cum_psum"), sem("route_step")
        lane_hot_ready, table_psum = sem("lane_hot_ready"), sem("table_psum")
        gather_at_ready, scatter_at_ready = sem("gather_at_ready"), sem("scatter_at_ready")
        gathered = [sem(f"gathered{e}") for e in range(E)]
        xeT_psum, xeT_ready, up_psum, hid_ready = sem("xeT_psum"), sem("xeT_ready"), sem("up_psum"), sem("hid_ready")
        down_psum, yb_ready, ys_ready, scattered = sem("down_psum"), sem("yb_ready"), sem("ys_ready"), sem("scattered")

        z_bank = [bank[2], bank[3]]
        v_bank = [bank[4], bank[5]]
        xT_bank, q_bank = bank[6], bank[7]
        scores_bank = [bank[0], bank[1]]
        probsT_bank = [bank[2], bank[3]]
        pv_bank, x2T_bank, logits_bank = bank[4], bank[5], bank[6]
        cum_bank, table_bank = bank[7], bank[5]
        up_bank = [bank[0:2], bank[2:4]]
        xeT_bank = [bank[4], bank[6]]
        down_bank = [bank[5], bank[7]]
        logits_ps = logits_bank[:, 0:TB * E].rearrange("p (h e) -> p h e", h=TB)
        cum_ps = cum_bank[:, 0:T * TOP_K * E]
        kept_ps = cum_bank[:, T * TOP_K * E:T * TOP_K * E + E]
        table_ps = table_bank[:, 0:SLOT_TILES]

        block = ctx.enter_context(nc.Block())

        @block.sync
        def _(sp):
            def load_rows(dst, src, g, signal):
                sp.dma_start(dst[:, g * GT:(g + 1) * GT, :],
                             src[g * GT * P:(g + 1) * GT * P, :].rearrange("(t p) d -> p t d", p=P)).then_inc(signal[g], 16)

            def store_rows(b):
                sp.wait_ge(comb_ready, b + 1)
                sp.wait_ge(x2_ready, b + 1)
                sp.dma_start(x2_rows[1 + b * S:1 + (b + 1) * S, :].rearrange("(t p) d -> p t d", p=P),
                             rows[:, b * TB:(b + 1) * TB, :]).then_inc(rows_stored, 16)

            def load_ctx(g):
                cols = slice(g * GT * P, (g + 1) * GT * P)
                sp.dma_start(yT[:, cols], ctxT[:, cols]).then_inc(y_loaded[g], 16)

            for g in range(G):
                load_ctx(g)
                load_rows(x_in, x_rows, g, x_loaded)
            sp.dma_start(b2_all[:, :, :], b2.rearrange("e d -> (e d)").partition_broadcast(P)
                         .rearrange("p (e d) -> p e d", e=E)).then_inc(b2_loaded, 16)
            for i in range(4):
                es = slice(i * E // 4, (i + 1) * E // 4)
                sp.dma_start(w1[:, es, :], W1[es].rearrange("e d h -> d e h")).then_inc(w1_loaded[i], 16)
                for e in range(i * E // 4, (i + 1) * E // 4):
                    sp.dma_start(w2[:, e, :, :], W2[e].rearrange("(c p) d -> p c d", p=P)).then_inc(w2_loaded[i], 16)
            sp.wait_ge(zeros_ready, 1)
            sp.dma_start(x2_rows[0:1, :], zeros[0:1, 0:ROW]).then_inc(pads_stored, 16)
            sp.dma_start(out[0:PAD, :].rearrange("(t p) d -> p t d", p=P),
                         zeros[:, 0:PAD // P * D].rearrange("p (t d) -> p t d", d=D)).then_inc(pads_stored, 16)
            for b in range(B):
                ts = slice(b * TB, (b + 1) * TB)
                sp.wait_ge(x1_ready, b + 1)
                sp.dma_start(out[PAD + b * S:PAD + (b + 1) * S, :].rearrange("(t p) d -> p t d", p=P),
                             x1[:, ts, :]).then_inc(x1_stored, 16)
                if b >= 1:
                    store_rows(b - 1)
            store_rows(B - 1)
            sp.wait_ge(x1_stored, 16 * B)
            sp.wait_ge(pads_stored, 32)
            sp.wait_ge(scattered, 16 * SLOT_TILES)

        @block.gpsimd
        def _(pool):
            pool.memset(ident[:, :], 0.0).then_inc(pool_step, 1)
            pool.memset(tri[:, :], 1.0).then_inc(pool_step, 1)
            pool.memset(ones[:, :], 1.0).then_inc(consts_ready, 1)
            pool.memset(neg_half[:, :], -0.5).then_inc(consts_ready, 1)
            pool.wait_ge(pool_step, 2)
            pool.affine_select(out=ident[:, :], in_=ident[:, :], compare_op=ALU.not_equal, fill=1.0, base=0,
                               pattern=[[-1, P]], channel_multiplier=1).then_inc(consts_ready, 1)
            pool.affine_select(out=tri[:, :], in_=tri[:, :], compare_op=ALU.is_ge, fill=0.0, base=0,
                               pattern=[[1, P]], channel_multiplier=-1).then_inc(consts_ready, 1)
            pool.memset(before[:, 0, :], 0.0).then_inc(consts_ready, 1)
            small = dict(allow_small_or_imprecise_dtypes=True)
            pool.iota(lane_iota[:, :, :], [[1, P], [0, QUAD]], base=1, channel_multiplier=0, **small).then_inc(consts_ready, 1)
            pool.iota(tile_iota[:, :, :], [[1, SLOT_TILES], [0, QUAD]], base=0, channel_multiplier=0, **small).then_inc(consts_ready, 1)
            pool.iota(expert_iota[:, :], [[1, E]], base=0, channel_multiplier=0, **small).then_inc(consts_ready, 1)
            pool.iota(token_no[:, :, :], [[P, T], [0, TOP_K]], base=1, channel_multiplier=1, **small).then_inc(consts_ready, 1)
            pool.iota(pad_row[:, :].rearrange("p (e s) -> p e s", s=ST), [[0, E], [P, ST]], base=-(PAD - 1),
                      channel_multiplier=1, **small).then_inc(consts_ready, 1)
            pool.memset(zeros[:, :], 0.0).then_inc(zeros_ready, 1)

            def inv_std(mv, rstd, t0, n, var_sem, rstd_sem, k):
                pool.tensor_scalar(rstd[:, t0:t0 + n], mv[:, t0:t0 + n, 1], LN_EPS, None, ALU.add).then_inc(var_sem, 1)
                pool.wait_ge(var_sem, k)
                pool.tensor_tensor(rstd[:, t0:t0 + n], rstd[:, t0:t0 + n], neg_half[:, 0:n], ALU.pow).then_inc(rstd_sem, 1)
                pool.wait_ge(rstd_sem, k)

            def inv_std1(g):
                pool.wait_ge(mv1_ready, g + 1)
                inv_std(mv1, rstd1, g * GT, GT, var1_ready, rstd1_ready, g + 1)

            def fraction(g):
                if g >= 2:
                    pool.wait_ge(khat_ready, g - 1)
                pool.wait_ge(whole_ready, g + 1)
                pool.tensor_tensor(frac[:, g % 2, :], turns[:, g % 2, :], whole[:, g % 2, :],
                                   ALU.subtract).then_inc(frac_ready, 1)

            def add_bv(g):
                pool.wait_ge(xn_ready, g + 1)
                ts = slice(g * GT, (g + 1) * GT)
                pool.tensor_tensor(x_in[:, ts, :], x_in[:, ts, :],
                                   gated_bv[:, :].unsqueeze(1).broadcast_to([P, GT, D]), ALU.add).then_inc(xb_ready, 1)

            inv_std1(0)
            inv_std1(1)
            fraction(0)
            inv_std1(2)
            fraction(1)
            inv_std1(3)
            fraction(2)
            fraction(3)
            pool.wait_ge(tanh_ready, 1)
            pool.wait_ge(bv_loaded, 16)
            pool.tensor_scalar(gated_bv[:, :], bv_all[:, :], tgates[:, 0:1], None, ALU.mult).then_inc(gated_bv_ready, 1)
            pool.wait_ge(gated_bv_ready, 1)
            add_bv(0)

            def norm2(b):
                pool.wait_ge(mv2_ready, b + 1)
                inv_std(mv2, rstd2, b * TB, TB, var2_ready, rstd2_ready, b + 1)
                if b == B - 1:
                    return
                ts = slice(b * TB, (b + 1) * TB)
                if b:
                    pool.wait_ge(x2_ready, b)
                pool.tensor_tensor(centred[:, :, :], x1[:, ts, :], mv2[:, ts, 0:1].broadcast_to([P, TB, D]),
                                   ALU.subtract).then_inc(centred_ready, 1)
                pool.wait_ge(centred_ready, b + 1)
                pool.tensor_tensor(rows[:, ts, 0:D], centred[:, :, :], rstd2[:, ts].unsqueeze(2).broadcast_to([P, TB, D]),
                                   ALU.mult).then_inc(x2_ready, 1)

            def count(b):
                pool.wait_ge(onehot_ready, b + 1)
                for t in range(b * TB, (b + 1) * TB):
                    if t:
                        pool.wait_ge(before_ready, t)
                    pool.tensor_tensor(before[:, t + 1, :], before[:, t, :],
                                       onehot[:, t, :, :].rearrange("p k e -> p (k e)"), ALU.add).then_inc(before_ready, 1)

            def gaps(i):
                b0, b1 = ROUTE_GROUPS[i]
                ts, n = slice(b0 * TB, b1 * TB), (b1 - b0) * TB
                pool.wait_ge(top_ready, b1)
                pool.tensor_tensor(top_diff[:, ts, :], top[:, ts, :], top[:, ts, 0:1].broadcast_to([P, n, 8]),
                                   ALU.subtract).then_inc(diff_ready, 1)

            def weights(i):
                b0, b1 = ROUTE_GROUPS[i]
                ts, n = slice(b0 * TB, b1 * TB), (b1 - b0) * TB
                k = 4 * i
                pool.wait_ge(w_rec_ready, i + 1)
                pool.tensor_tensor(w_top[:, ts, 0], w_den[:, ts], tgates[:, 1:2].broadcast_to([P, n]),
                                   ALU.mult).then_inc(weight_step, 1)
                pool.wait_ge(weight_step, k + 1)
                pool.tensor_tensor(w_top[:, ts, 1], w_top[:, ts, 0], top_exp[:, ts, 1], ALU.mult).then_inc(weight_step, 1)
                pool.tensor_tensor(comb0[:, ts, :], onehot[:, ts, 0, :], w_top[:, ts, 0:1].broadcast_to([P, n, E]),
                                   ALU.mult).then_inc(weight_step, 1)
                pool.wait_ge(weight_step, k + 3)
                pool.tensor_tensor(comb1[:, ts, :], onehot[:, ts, 1, :], w_top[:, ts, 1:2].broadcast_to([P, n, E]),
                                   ALU.mult).then_inc(weight_step, 1)
                pool.wait_ge(weight_step, k + 4)
                pool.tensor_tensor(rows[:, ts, D:ROW], comb0[:, ts, :], comb1[:, ts, :], ALU.add)\
                    .then_inc(comb_ready, b1 - b0)

            for s in range(B + 4):
                if 1 <= s <= B:
                    norm2(s - 1)
                if s + 1 < G:
                    add_bv(s + 1)
                if 3 <= s < B + 3:
                    count(s - 3)
                for i, (b0, b1) in enumerate(ROUTE_GROUPS):
                    if s == b1 + 2:
                        gaps(i)
                    if s == b1 + 3:
                        weights(i)

            def gather(j):
                pool.indirect_dma_start(out=xe[:, j, :], out_offset=None, in_=x2_rows[:, :],
                                        in_offset=bass.IndirectOffsetOnAxis(ap=gather_at[:, j:j + 1], axis=0))\
                    .then_inc(gathered[j // ST], 16)

            AHEAD = 4 * ST
            pool.wait_ge(rows_stored, 16 * B)
            pool.wait_ge(pads_stored, 32)
            pool.wait_ge(gather_at_ready, 1)
            for j in range(AHEAD):
                gather(j)
            pool.wait_ge(scatter_at_ready, 1)
            pool.wait_ge(x1_stored, 16 * B)
            for e in range(E):
                pool.wait_ge(ys_ready, e + 1)
                if e:
                    pool.wait_ge(scattered, 16 * ST * e)
                for j in range(e * ST, (e + 1) * ST):
                    pool.indirect_dma_start(out=out[:, :],
                                            out_offset=bass.IndirectOffsetOnAxis(ap=scatter_at[:, j:j + 1], axis=0),
                                            in_=ys[:, e % 2, j % ST, :], in_offset=None,
                                            compute_op=ALU.add).then_inc(scattered, 16)
                for j in range(e * ST + AHEAD, min((e + 1) * ST + AHEAD, SLOT_TILES)):
                    gather(j)

        @block.scalar
        def _(act):
            act.dma_start(keys_in[:, :], key_pack).then_inc(keys_loaded, 16)
            act.dma_start(gates[:, :], gates_in.partition_broadcast(P)).then_inc(gates_loaded, 16)
            act.dma_start(projs_in[:, :], proj_pack).then_inc(projs_loaded, 16)
            act.dma_start(bv_all[:, :], bv.partition_broadcast(P)).then_inc(bv_loaded, 16)
            act.wait_ge(gates_loaded, 16)
            act.activation(tgates[:, :], gates[:, :], ACT.Tanh).then_inc(tanh_ready, 1)

            def copy_turns(g):
                act.wait_ge(z_psum, g + 1)
                if g >= 2:
                    act.wait_ge(frac_ready, g - 1)
                else:
                    act.wait_ge(turn_ready, 1)
                act.activation(turns[:, g % 2, :], z_bank[g % 2][:, :], ACT.Identity, bias=turn[:, 0:1])\
                    .then_inc(turns_ready, 1)

            def copy_xT(g):
                act.wait_ge(xT_psum, g + 1)
                if g >= 2:
                    act.wait_ge(q_psum, g - 1)
                act.activation(xnT[:, g % 2, :], xT_bank[:, :], ACT.Copy).then_inc(xT_ready, 1)

            def copy_v(g):
                act.wait_ge(v_psum, g + 1)
                act.activation(v[:, g * GT:(g + 1) * GT, :].rearrange("p t d -> p (t d)"), v_bank[g % 2][:, :],
                               ACT.Copy, scale=tgates[:, 0:1]).then_inc(v_ready, 1)

            def cosine(g):
                act.wait_ge(frac_ready, g + 1)
                act.activation(khatT[:, g * GT * P:(g + 1) * GT * P], frac[:, g % 2, :], ACT.Sin,
                               scale=SIN_SCALE).then_inc(khat_ready, 1)

            act.wait_ge(tanh_ready, 1)
            copy_turns(0)
            copy_v(0)
            copy_turns(1)
            copy_v(1)
            copy_xT(0)
            cosine(0)
            copy_turns(2)
            copy_v(2)
            copy_xT(1)
            cosine(1)
            copy_turns(3)
            copy_v(3)
            copy_xT(2)
            cosine(2)
            copy_xT(3)
            cosine(3)

            for s in range(B + 4):
                if 1 <= s <= B:
                    b = s - 1
                    act.wait_ge(probsT_psum, b + 1)
                    if b >= 2:
                        act.wait_ge(pv_psum, b - 1)
                    act.activation(probsT[:, b % 2, :, :].rearrange("p h q -> p (h q)"), probsT_bank[b % 2][:, :],
                                   ACT.Copy).then_inc(probsT_ready, 1)
                if 3 <= s < B + 3:
                    b = s - 3
                    act.wait_ge(x2T_psum, b + 1)
                    if b >= 2:
                        act.wait_ge(logits_psum, b - 1)
                    act.activation(x2T[:, b % 2, :], x2T_bank[:, 0:TB * P], ACT.Copy).then_inc(x2T_ready, 1)
                if s < B:
                    act.wait_ge(max_ready, s + 1)
                    if s >= 2:
                        act.wait_ge(probsT_psum, s - 1)
                    for h in range(TB):
                        act.activation(probs[:, s % 2, h, :], scores_bank[s % 2][:, h * S:(h + 1) * S], ACT.Exp,
                                       bias=neg_max[:, s, h:h + 1], accum_out=den[:, s, h:h + 1]).then_inc(probs_ready, 1)
                for i, (b0, b1) in enumerate(ROUTE_GROUPS):
                    if s == b1 + 3:
                        ts = slice(b0 * TB, b1 * TB)
                        act.wait_ge(diff_ready, i + 1)
                        act.activation(top_exp[:, ts, :], top_diff[:, ts, :], ACT.Exp).then_inc(exp_ready, 1)

            for e in range(E):
                if e >= 2:
                    act.wait_ge(down_psum, e - 1)
                for c in range(C):
                    act.wait_ge(up_psum, e * (C // 2) + c // 2 + 1)
                    last = act.activation(hid[:, e % 2, c, :],
                                          up_bank[e % 2][c // 2][:, c % 2 * CAPACITY:(c % 2 + 1) * CAPACITY],
                                          ACT.Gelu_apprx_tanh, bias=bias_cols[:, e * C + c:e * C + c + 1])
                    if c % 2:
                        last.then_inc(hid_ready, 1)

        @block.tensor
        def _(pe):
            def turn_x(g):
                if g == 0:
                    pe.wait_ge(consts_ready, CONSTS)
                pe.wait_ge(xn_ready, g + 1)
                if g:
                    pe.wait_ge(xT_ready, g)
                else:
                    pe.wait_ge(wkr_ready, 1)
                for i in range(GT):
                    last = pe.transpose(xT_bank[:, i * P:(i + 1) * P], xn[:, g % 2, i, :], ident[:, :])
                last.then_inc(xT_psum, 1)

            def keys(g):
                pe.wait_ge(y_loaded[g], 16)
                pe.wait_ge(wkr_ready, 1)
                if g >= 2:
                    pe.wait_ge(turns_ready, g - 1)
                pe.matmul(z_bank[g % 2][:, :], wkr[:, :], yT[:, g * GT * P:(g + 1) * GT * P],
                          start=True, stop=True).then_inc(z_psum, 1)
                pe.wait_ge(projs_loaded, 16)
                if g >= 2:
                    pe.wait_ge(v_ready, g - 1)
                for i in range(GT):
                    last = pe.matmul(v_bank[g % 2][:, i * D:(i + 1) * D], yT[:, (g * GT + i) * P:(g * GT + i + 1) * P], wv,
                                     start=True, stop=True)
                last.then_inc(v_psum, 1)

            def queries(g):
                pe.wait_ge(xT_ready, g + 1)
                if g:
                    pe.wait_ge(q_ready, g)
                else:
                    pe.wait_ge(turn0_ready, 1)
                pe.matmul(q_bank[:, :], wq, xnT[:, g % 2, :], start=True, stop=True).then_inc(q_psum, 1)

            pe.wait_ge(keys_loaded, 16)
            pe.matmul(xT_bank[:, 0:P], wkT, wr, start=True, stop=True).then_inc(wkr_psum, 1)
            pe.matmul(q_bank[:, 0:1], wr, bias_cols[:, BK:BK + 1], start=True, stop=True).then_inc(turn_psum, 1)
            keys(0)
            keys(1)
            turn_x(0)
            queries(0)
            keys(2)
            turn_x(1)
            queries(1)
            keys(3)
            turn_x(2)
            queries(2)
            turn_x(3)
            queries(3)

            for s in range(B + 3):
                if s < B:
                    g = s // GB
                    pe.wait_ge(khat_ready, g + 1)
                    pe.wait_ge(q_ready, g + 1)
                    if s >= 2:
                        pe.wait_ge(probs_ready, TB * (s - 1))
                    for h in range(TB):
                        q0 = s * S + h * P
                        last = pe.matmul(scores_bank[s % 2][:, h * S:(h + 1) * S], qT[:, q0:q0 + P],
                                         khatT[:, s * S:(s + 1) * S], start=True, stop=True)
                    last.then_inc(scores_psum, 1)
                if 1 <= s <= B:
                    b = s - 1
                    pe.wait_ge(probs_ready, TB * (b + 1))
                    if b >= 2:
                        pe.wait_ge(probsT_ready, b - 1)
                    for k in range(TB):
                        for h in range(TB):
                            c0 = k * S + h * P
                            last = pe.transpose(probsT_bank[b % 2][:, c0:c0 + P], probs[:, b % 2, h, k * P:(k + 1) * P],
                                                ident[:, :])
                    last.then_inc(probsT_psum, 1)
                if 3 <= s:
                    b = s - 3
                    pe.wait_ge(x2_ready, b + 1)
                    if b:
                        pe.wait_ge(x2T_ready, b)
                    for h in range(TB):
                        last = pe.transpose(x2T_bank[:, h * P:(h + 1) * P], rows[:, b * TB + h, 0:D], ident[:, :])
                    last.then_inc(x2T_psum, 1)
                if 1 <= s <= B:
                    b = s - 1
                    pe.wait_ge(probsT_ready, b + 1)
                    pe.wait_ge(v_ready, b // GB + 1)
                    if b:
                        pe.wait_ge(x1_ready, b)
                    for h in range(TB):
                        for k in range(TB):
                            last = pe.matmul(pv_bank[:, h * D:(h + 1) * D], probsT[:, b % 2, k, h * P:(h + 1) * P],
                                             v[:, b * TB + k, :], start=(k == 0), stop=(k == TB - 1))
                    last.then_inc(pv_psum, 1)
                if 3 <= s:
                    b = s - 3
                    pe.wait_ge(x2T_ready, b + 1)
                    if b:
                        pe.wait_ge(top_at_ready, b)
                    for h in range(TB):
                        last = pe.matmul(logits_ps[:, h, :], x2T[:, b % 2, h * P:(h + 1) * P], wg,
                                         start=True, stop=True)
                    last.then_inc(logits_psum, 1)

            pe.wait_ge(before_ready, T)
            pe.matmul(cum_ps, tri[:, :], onehot[:, :, :, :].rearrange("p t k e -> p (t k e)"), start=True, stop=False)
            pe.matmul(cum_ps, ones[:, :], before[:, 0:T, :].rearrange("p t c -> p (t c)"), start=False, stop=True)
            pe.matmul(kept_ps, ones[:, :], before[:, T, 0:E], start=True, stop=True).then_inc(cum_psum, 1)
            for n in range(T * TOP_K):
                pe.wait_ge(lane_hot_ready, n + 1)
                last = pe.matmul(table_ps, lane_hot[:, n // QUAD, :, n % QUAD], token_hot[:, n // QUAD, :, n % QUAD], start=(n == 0), stop=(n == T * TOP_K - 1))
            last.then_inc(table_psum, 1)

            def turn_xe(e):
                pe.wait_ge(gathered[e], 16 * ST)
                if e >= 2:
                    pe.wait_ge(xeT_ready, e - 1)
                for h in range(ST):
                    last = pe.transpose(xeT_bank[e % 2][:, h * P:(h + 1) * P], xe[:, e * ST + h, 0:D], ident[:, :])
                last.then_inc(xeT_psum, 1)

            def up(e):
                if e % 2 == 0:
                    pe.wait_ge(w1_loaded[e // 2], 16)
                pe.wait_ge(xeT_ready, e + 1)
                for c in range(C):
                    if e >= 2 and c % 2 == 0:
                        pe.wait_ge(hid_ready, (e - 2) * (C // 2) + c // 2 + 1)
                    last = pe.matmul(up_bank[e % 2][c // 2][:, c % 2 * CAPACITY:(c % 2 + 1) * CAPACITY],
                                     w1[:, e, c * P:(c + 1) * P], xeT[:, e % 2, :], start=True, stop=True)
                    if c % 2:
                        last.then_inc(up_psum, 1)

            def down(e):
                if e % 2 == 0:
                    pe.wait_ge(w2_loaded[e // 2], 32)
                pe.wait_ge(hid_ready, (e + 1) * (C // 2))
                if e >= 2:
                    pe.wait_ge(yb_ready, e - 1)
                else:
                    pe.wait_ge(scatter_at_ready, 1)
                for h in range(ST):
                    for c in range(C):
                        last = pe.matmul(down_bank[e % 2][:, h * D:(h + 1) * D], hid[:, e % 2, c, h * P:(h + 1) * P],
                                         w2[:, e, c, :], start=(c == 0), stop=(c == C - 1))
                last.then_inc(down_psum, 1)

            turn_xe(0)
            for e in range(E + 1):
                if e < E:
                    up(e)
                if e + 1 < E:
                    turn_xe(e + 1)
                if e:
                    down(e - 1)

        @block.vector
        def _(dve):
            def stats(src, st, mv, t0, n, st_sem, mv_sem, k):
                for t in range(t0, t0 + n):
                    last = dve.bn_stats(st[:, t, :], src[:, t, :])
                last.then_inc(st_sem, 1)
                dve.wait_ge(st_sem, k)
                for t in range(t0, t0 + n):
                    last = dve.bn_aggr(mv[:, t, :], st[:, t, :])
                last.then_inc(mv_sem, 1)

            def stats_x(g):
                dve.wait_ge(x_loaded[g], 16)
                stats(x_in, stats1, mv1, g * GT, GT, stats1_ready, mv1_ready, g + 1)

            def normalise(g):
                dve.wait_ge(rstd1_ready, g + 1)
                if g >= 2:
                    dve.wait_ge(xT_psum, g - 1)
                for i in range(GT):
                    t = g * GT + i
                    last = dve.tensor_scalar(xn[:, g % 2, i, :], x_in[:, t, :], mv1[:, t, 0:1], rstd1[:, t:t + 1],
                                             ALU.subtract, ALU.mult)
                last.then_inc(xn_ready, 1)

            def round_turns(g):
                dve.wait_ge(turns_ready, g + 1)
                if g >= 2:
                    dve.wait_ge(frac_ready, g - 1)
                dve.tensor_scalar(whole[:, g % 2, :], turns[:, g % 2, :], ROUND_MAGIC, ROUND_MAGIC,
                                  ALU.add, ALU.subtract).then_inc(whole_ready, 1)

            def copy_q(g):
                dve.wait_ge(q_psum, g + 1)
                dve.tensor_scalar(qT[:, g * GT * P:(g + 1) * GT * P], q_bank[:, :], bias_cols[:, BQ:BQ + 1], None,
                                  ALU.add).then_inc(q_ready, 1)

            dve.wait_ge(wkr_psum, 1)
            dve.tensor_scalar(wkr[:, :], xT_bank[:, 0:P], 1.0 / TWO_PI, None, ALU.mult).then_inc(wkr_ready, 1)
            dve.wait_ge(turn_psum, 1)
            dve.tensor_scalar(turn0[:, :], q_bank[:, 0:1], bias_cols[:, BR:BR + 1], None, ALU.add).then_inc(turn0_ready, 1)
            dve.wait_ge(turn0_ready, 1)
            dve.tensor_scalar(turn[:, :], turn0[:, :], 1.0 / TWO_PI, 0.25, ALU.mult, ALU.add).then_inc(turn_ready, 1)
            stats_x(0)
            stats_x(1)
            normalise(0)
            round_turns(0)
            stats_x(2)
            normalise(1)
            round_turns(1)
            copy_q(0)
            stats_x(3)
            normalise(2)
            round_turns(2)
            copy_q(1)
            normalise(3)
            round_turns(3)
            copy_q(2)
            copy_q(3)

            def scores_max(b):
                dve.wait_ge(scores_psum, b + 1)
                dve.tensor_reduce(neg_max[:, b, :], scores_bank[b % 2][:, :].rearrange("p (h k) -> p h k", h=TB), AX.X,
                                  ALU.max, negate=True).then_inc(max_ready, 1)

            def residual(b):
                dve.wait_ge(rden_ready, b + 1)
                dve.wait_ge(xb_ready, b // GB + 1)
                dve.wait_ge(pv_psum, b + 1)
                for h in range(TB):
                    t = b * TB + h
                    last = dve.scalar_tensor_tensor(out=x1[:, t, :], in0=pv_bank[:, h * D:(h + 1) * D],
                                                    scalar=rden[:, b, h:h + 1], in1=x_in[:, t, :],
                                                    op0=ALU.mult, op1=ALU.add)
                last.then_inc(x1_ready, 1)

            def route_top(b):
                dve.wait_ge(logits_psum, b + 1)
                for h in range(TB):
                    last = dve.max(top[:, b * TB + h, :], logits_ps[:, h, :])
                last.then_inc(top_ready, 1)

            def route_at(b):
                dve.wait_ge(top_ready, b + 1)
                for h in range(TB):
                    last = dve.max_index(top_at[:, b * TB + h, :], top[:, b * TB + h, :], logits_ps[:, h, :])
                last.then_inc(top_at_ready, 1)

            def route_onehot(b):
                ts = slice(b * TB, (b + 1) * TB)
                dve.wait_ge(top_at_ready, b + 1)
                dve.tensor_tensor(onehot[:, ts, :, :],
                                  expert_iota[:, :].unsqueeze(1).unsqueeze(1).broadcast_to([P, TB, TOP_K, E]),
                                  top_at[:, ts, 0:TOP_K].unsqueeze(3).broadcast_to([P, TB, TOP_K, E]),
                                  ALU.is_equal).then_inc(onehot_ready, 1)

            def weight_recip(i):
                b0, b1 = ROUTE_GROUPS[i]
                ts = slice(b0 * TB, b1 * TB)
                dve.wait_ge(exp_ready, i + 1)
                dve.tensor_reduce(exp_sum[:, ts], top_exp[:, ts, :], AX.X, ALU.add).then_inc(exp_sum_ready, 1)
                dve.wait_ge(exp_sum_ready, i + 1)
                dve.scalar_tensor_tensor(out=w_den[:, ts], in0=exp_sum[:, ts], scalar=WEIGHT_EPS, in1=top_exp[:, ts, 1],
                                         op0=ALU.mult, op1=ALU.add).then_inc(w_den_ready, 1)
                dve.wait_ge(w_den_ready, 2 * i + 1)
                dve.tensor_scalar(w_den[:, ts], w_den[:, ts], 1.0, None, ALU.add).then_inc(w_den_ready, 1)
                dve.wait_ge(w_den_ready, 2 * i + 2)
                dve.reciprocal(w_den[:, ts], w_den[:, ts]).then_inc(w_rec_ready, 1)

            dve.wait_ge(consts_ready, CONSTS)
            for s in range(B + 4):
                if 1 <= s <= B:
                    dve.wait_ge(probs_ready, TB * s)
                    dve.reciprocal(rden[:, s - 1, :], den[:, s - 1, :]).then_inc(rden_ready, 1)
                if s < B:
                    scores_max(s)
                if 1 <= s <= B:
                    b = s - 1
                    residual(b)
                if 3 <= s < B + 3:
                    route_top(s - 3)
                if 1 <= s <= B:
                    dve.wait_ge(x1_ready, b + 1)
                    for t in range(b * TB, (b + 1) * TB):
                        last = dve.bn_stats(stats2[:, t, :], x1[:, t, :])
                    last.then_inc(stats2_ready, 1)
                if 3 <= s < B + 3:
                    route_at(s - 3)
                if 1 <= s <= B:
                    dve.wait_ge(stats2_ready, b + 1)
                    for t in range(b * TB, (b + 1) * TB):
                        last = dve.bn_aggr(mv2[:, t, :], stats2[:, t, :])
                    last.then_inc(mv2_ready, 1)
                if 3 <= s < B + 3:
                    route_onehot(s - 3)
                if s == B:
                    dve.wait_ge(rstd2_ready, B)
                    for t in range(b * TB, (b + 1) * TB):
                        last = dve.tensor_scalar(rows[:, t, 0:D], x1[:, t, :], mv2[:, t, 0:1], rstd2[:, t:t + 1],
                                                 ALU.subtract, ALU.mult)
                    last.then_inc(x2_ready, 1)
                for i, (b0, b1) in enumerate(ROUTE_GROUPS[:-1]):
                    if s == b1 + 3:
                        weight_recip(i)

            step = 0

            def chain(last):
                nonlocal step
                step += 1
                last.then_inc(route_step, 1)
                return step

            pairs = lambda a: a[:, :].rearrange("p (t k) -> p t k", k=TOP_K)
            dve.wait_ge(cum_psum, 1)
            dve.wait_ge(onehot_ready, B)
            n_picked = chain(dve.tensor_tensor(picked[:, :, :], onehot[:, :, :, :].rearrange("p t k e -> p (t k) e"),
                                               cum_ps.rearrange("p (n e) -> p n e", e=E), ALU.mult))
            n_kept = chain(dve.tensor_scalar(kept1[:, :], kept_ps, float(CAPACITY), None, ALU.min))
            dve.wait_ge(route_step, n_picked)
            n_pos = chain(dve.tensor_reduce(pos[:, :], picked[:, :, :], AX.X, ALU.add))
            weight_recip(len(ROUTE_GROUPS) - 1)
            dve.wait_ge(route_step, n_kept)
            n_picked1 = chain(dve.tensor_tensor(picked1[:, :, :], onehot[:, :, 1, :],
                                                kept1[:, :].unsqueeze(1).broadcast_to([P, T, E]), ALU.mult))
            dve.wait_ge(route_step, n_picked1)
            n_shift = chain(dve.tensor_reduce(shift1[:, :], picked1[:, :, :], AX.X, ALU.add))
            dve.wait_ge(route_step, n_shift)
            n_pos = chain(dve.tensor_tensor(pairs(pos)[:, :, 1], pairs(pos)[:, :, 1], shift1[:, :], ALU.add))
            dve.wait_ge(route_step, n_pos)
            n_upper = chain(dve.tensor_scalar(upper[:, :], pos[:, :], float(P), None, ALU.is_gt))
            n_over = chain(dve.tensor_scalar(over[:, :], pos[:, :], float(CAPACITY), float(SLOT_TILES), ALU.is_gt, ALU.mult))
            dve.wait_ge(route_step, n_upper)
            n_lane = chain(dve.scalar_tensor_tensor(out=lane[:, :], in0=upper[:, :], scalar=-float(P), in1=pos[:, :],
                                                    op0=ALU.mult, op1=ALU.add))
            dve.wait_ge(route_step, n_over)
            n_up = chain(dve.tensor_tensor(upper[:, :], upper[:, :], over[:, :], ALU.add))
            dve.wait_ge(route_step, n_up)
            n_tile = chain(dve.scalar_tensor_tensor(out=pairs(slot_tile), in0=top_at[:, :, 0:TOP_K], scalar=float(ST),
                                                    in1=pairs(upper), op0=ALU.mult, op1=ALU.add))
            dve.wait_ge(route_step, n_tile)
            quads = lambda a, m: (a[:, :].rearrange("p (g q) -> p g q", q=QUAD).unsqueeze(2)
                                  .broadcast_to([P, QUADS, m, QUAD]))
            n_hot = chain(dve.tensor_tensor(tile_hot[:, :, :, :],
                                            tile_iota[:, :, :].unsqueeze(1).broadcast_to([P, QUADS, SLOT_TILES, QUAD]),
                                            quads(slot_tile, SLOT_TILES), ALU.is_equal))
            dve.wait_ge(route_step, n_hot)
            chain(dve.tensor_tensor(token_hot[:, :, :, :], tile_hot[:, :, :, :],
                                    quads(token_no[:, :, :].rearrange("p t k -> p (t k)"), SLOT_TILES), ALU.mult))
            for g in range(0, QUADS, 2):
                gs = slice(g, g + 2)
                dve.tensor_tensor(lane_hot[:, gs, :, :], lane_iota[:, :, :].unsqueeze(1).broadcast_to([P, 2, P, QUAD]),
                                  quads(lane, P)[:, gs, :, :], ALU.is_equal).then_inc(lane_hot_ready, 2 * QUAD)
            dve.wait_ge(table_psum, 1)
            dve.tensor_copy(gather_at[:, :], table_ps).then_inc(gather_at_ready, 1)
            n_empty = chain(dve.tensor_scalar(empty[:, :], table_ps, 0.0, None, ALU.is_equal))
            dve.wait_ge(route_step, n_empty)
            n_row = chain(dve.tensor_tensor(empty_row[:, :], empty[:, :], pad_row[:, :], ALU.mult))
            dve.wait_ge(route_step, n_row)
            dve.scalar_tensor_tensor(out=scatter_at[:, :], in0=table_ps, scalar=float(PAD - 1), in1=empty_row[:, :],
                                     op0=ALU.add, op1=ALU.add).then_inc(scatter_at_ready, 1)

            def copy_xeT(e):
                dve.wait_ge(xeT_psum, e + 1)
                if e >= 2:
                    dve.wait_ge(up_psum, (e - 1) * (C // 2))
                dve.tensor_copy(xeT[:, e % 2, :], xeT_bank[e % 2][:, 0:CAPACITY]).then_inc(xeT_ready, 1)

            def weigh(e):
                dve.wait_ge(down_psum, e + 1)
                if e == 0:
                    dve.wait_ge(b2_loaded, 16)
                dve.tensor_tensor(yb[:, e % 2, :, :], down_bank[e % 2][:, 0:ST * D].rearrange("p (s d) -> p s d", s=ST),
                                  b2_all[:, e, :].unsqueeze(1).broadcast_to([P, ST, D]), ALU.add).then_inc(yb_ready, 1)
                dve.wait_ge(yb_ready, e + 1)
                if e >= 2:
                    dve.wait_ge(scattered, 16 * ST * (e - 1))
                for h in range(ST):
                    last = dve.tensor_scalar(ys[:, e % 2, h, :], yb[:, e % 2, h, :], xe[:, e * ST + h, D + e:D + e + 1],
                                             None, ALU.mult)
                last.then_inc(ys_ready, 1)

            copy_xeT(0)
            for e in range(E + 1):
                if e + 1 < E:
                    copy_xeT(e + 1)
                if e:
                    weigh(e - 1)


def _lay_out(inputs):
    col = lambda name: inputs["L0_xattn_" + name][:, None]
    x, ctx = inputs["x"], inputs["ctx_1024"]
    W1, b1 = inputs["L0_ffn_W1"], inputs["L0_ffn_b1"]
    return {
        "x": x,
        "ctxT": ctx.reshape(-1, ctx.shape[-1]).T,
        "gates": np.concatenate([inputs["g_xattn"], inputs["g_ffn"]]),
        "keys": np.concatenate([inputs["L0_xattn_Wk"].T, inputs["L0_xattn_Wr"], b1.reshape(-1, x.shape[-1]).T,
                                col("bq"), col("bk"), col("br")], axis=1),
        "projs": np.concatenate([inputs["L0_xattn_Wv"], inputs["L0_xattn_Wq"], inputs["L0_ffn_Wg"]], axis=1),
        "bv": inputs["L0_xattn_bv"],
        "W1": W1,
        "W2": inputs["L0_ffn_W2"],
        "b2": inputs["L0_ffn_b2"],
    }


def kernel(**inputs):
    import concourse.bacc as _bacc
    from concourse.bass_utils import run_bass_kernel_spmd as _run

    nc = _bacc.Bacc("TRN2", target_bir_lowering=False, num_devices=1)
    inputs = {name: np.asarray(a) for name, a in inputs.items()}
    arrays, args = {}, []
    for name, a in _lay_out(inputs).items():
        a = np.ascontiguousarray(a)
        arrays[f"in_{name}"] = a
        args.append(nc.dram_tensor(f"in_{name}", a.shape, mybir.dt.from_np(a.dtype), kind="ExternalInput").ap())
    B, S, D = inputs["x"].shape
    E = inputs["L0_ffn_W1"].shape[0]
    out = nc.dram_tensor("out", (CAPACITY + B * S, D), F32, kind="ExternalOutput").ap()
    x2_rows = nc.dram_tensor("x2_rows", (1 + B * S, D + E), F32, kind="Internal").ap()
    build(nc, *args, out, x2_rows)
    r = _run(nc, [arrays], core_ids=[0])
    return r.results[0]["out"][CAPACITY:].reshape(B, S, D)
```

```python
from contextlib import ExitStack

import numpy as np
import concourse.bass as bass
from concourse import mybir

F32 = mybir.dt.float32
F16 = mybir.dt.float16
I32 = mybir.dt.int32
U32 = mybir.dt.uint32
ALU = mybir.AluOpType
ACT = mybir.ActivationFunctionType
AX = mybir.AxisListType

P = 128
CAPACITY = 256
TOP_K = 2
LN_EPS = 1e-5
WEIGHT_EPS = 1e-9
TWO_PI = 6.283185307179586
SIN_SCALE = 6.283185
ROUND_MAGIC = 12582912.0


def build(nc, x, ctxT, gates_in, key_pack, proj_pack, bv, W1, W2, b2, out, x2_rows):
    B, S, D = x.shape
    E, _, H = W1.shape
    N = B * S
    T = N // P
    TB = S // P
    GT = 4
    G = T // GT
    GB = GT // TB
    C = H // P
    SLOT_TILES = E * CAPACITY // P
    ST = CAPACITY // P
    ROW = D + E
    TURN_P, PV, NORM2, TURN_X2, LOGITS, ROUTE = 1, 2, 3, 4, 5, 5
    STEPS = B + ROUTE + 2
    QUAD = 4
    QUADS = T * TOP_K // QUAD
    CONSTS = 9
    ROUTE_GROUPS = ((0, B // 2), (B // 2, B))
    WEIGHT_STEP = (B + 2, B + ROUTE)
    PAD = CAPACITY
    assert D == P and TB == 2 and ST == 2 and N <= 2048

    x_rows = x.rearrange("b s d -> (b s) d")

    ctx = ExitStack()
    with ctx:
        def sb(name, shape, dt=F32):
            return ctx.enter_context(nc.sbuf_tensor(name, shape, dt))

        def sem(name):
            return ctx.enter_context(nc.semaphore(name))

        bank = [ctx.enter_context(nc.psum_tensor(f"bank{i}", [P, 512], F32)) for i in range(8)]

        ident = sb("ident", [P, P])
        tri = sb("tri", [P, P], F16)
        ones = sb("ones", [P, P], F16)
        lane_iota = sb("lane_iota", [P, P, QUAD], F16)
        tile_iota = sb("tile_iota", [P, SLOT_TILES, QUAD], F16)
        expert_iota = sb("expert_iota", [P, E], F16)
        token_no = sb("token_no", [P, T, TOP_K], F16)
        pad_row = sb("pad_row", [P, SLOT_TILES])
        neg_half = sb("neg_half", [P, 8])
        zeros = sb("zeros", [P, 2 * ROW])
        BQ, BK, BR = E * C, E * C + 1, E * C + 2
        keys_in = sb("keys_in", [P, 2 * P + BR + 1])
        wkT, wr, bias_cols = keys_in[:, 0:P], keys_in[:, P:2 * P], keys_in[:, 2 * P:]
        projs_in = sb("projs_in", [P, 2 * P + E])
        wv, wq, wg = projs_in[:, 0:P], projs_in[:, P:2 * P], projs_in[:, 2 * P:]
        bv_all = sb("bv_all", [P, D])
        b2_all = sb("b2_all", [P, E, D])
        gates = sb("gates", [P, 2])
        tgates = sb("tgates", [P, 2])
        warm_sin = sb("warm_sin", [P, 2])
        gated_bv = sb("gated_bv", [P, D])
        wkr = sb("wkr", [P, P])
        turn0 = sb("turn0", [P, 1])
        turn = sb("turn", [P, 1])
        w1 = sb("w1", [P, E, H])
        w2 = sb("w2", [P, E, C, D])
        x_in = sb("x_in", [P, T, D])
        yT = sb("yT", [P, N])
        stats1 = sb("stats1", [P, T, 6])
        mv1 = sb("mv1", [P, T, 2])
        rstd1 = sb("rstd1", [P, T])
        xn = sb("xn", [P, 2, GT, D])
        xnT = sb("xnT", [P, 2, GT * P])
        qT = sb("qT", [P, N])
        turns = sb("turns", [P, 2, GT * P])
        whole = sb("whole", [P, 2, GT * P])
        frac = sb("frac", [P, 2, GT * P])
        khatT = sb("khatT", [P, N])
        v = sb("v", [P, T, D])
        neg_max = sb("neg_max", [P, B, TB])
        den = sb("den", [P, B, TB])
        rden = sb("rden", [P, B, TB])
        probs = sb("probs", [P, 2, TB, S])
        probsT = sb("probsT", [P, 2, TB, S])
        x1 = sb("x1", [P, T, D])
        stats2 = sb("stats2", [P, T, 6])
        mv2 = sb("mv2", [P, T, 2])
        rstd2 = sb("rstd2", [P, T])
        neg_mean2 = sb("neg_mean2", [P, T])
        shift2 = sb("shift2", [P, T])
        rows = sb("rows", [P, T, ROW])
        x2T = sb("x2T", [P, 2, TB * P])
        top = sb("top", [P, T, 8])
        top_at = sb("top_at", [P, T, 8], U32)
        top_diff = sb("top_diff", [P, T, 8])
        top_exp = sb("top_exp", [P, T, 8])
        exp_sum = sb("exp_sum", [P, T])
        exp_top = sb("exp_top", [P, T])
        w_den = sb("w_den", [P, T])
        w_top = sb("w_top", [P, T, TOP_K])
        onehot = sb("onehot", [P, T, TOP_K, E], F16)
        before = sb("before", [P, B, TOP_K * E], F16)
        pair_sum = sb("pair_sum", [P, TOP_K * E], F16)
        comb0 = sb("comb0", [P, T, E])
        comb1 = sb("comb1", [P, T, E])
        picked = sb("picked", [P, T * TOP_K, E])
        pos = sb("pos", [P, T * TOP_K])
        kept = sb("kept", [P, E], F16)
        upper = sb("upper", [P, T * TOP_K])
        first_tile = sb("first_tile", [P, T, TOP_K])
        warm_up = sb("warm_up", [P, 512], F16)
        lane = sb("lane", [P, T * TOP_K], F16)
        slot_tile = sb("slot_tile", [P, T * TOP_K], F16)
        lane_hot = sb("lane_hot", [P, QUADS, P, QUAD], F16)
        tile_hot = sb("tile_hot", [P, QUADS, SLOT_TILES, QUAD], F16)
        token_hot = sb("token_hot", [P, QUADS, SLOT_TILES, QUAD], F16)
        gather_at = sb("gather_at", [P, SLOT_TILES], I32)
        scatter_at = sb("scatter_at", [P, SLOT_TILES], I32)
        empty = sb("empty", [P, SLOT_TILES])
        empty_row = sb("empty_row", [P, SLOT_TILES])
        xe = sb("xe", [P, SLOT_TILES, ROW])
        xeT = sb("xeT", [P, 2, CAPACITY])
        hid = sb("hid", [P, 2, C, CAPACITY])
        weighed_b2 = sb("weighed_b2", [P, 2, ST, D])
        ys = sb("ys", [P, 2, ST, D])

        y_loaded = [sem(f"y_loaded{g}") for g in range(G)]
        x_loaded = [sem(f"x_loaded{g}") for g in range(G)]
        keys_loaded, projs_loaded = sem("keys_loaded"), sem("projs_loaded")
        gates_loaded = sem("gates_loaded")
        bv_loaded = sem("bv_loaded")
        b2_loaded = sem("b2_loaded")
        w1_loaded = [sem(f"w1_loaded{i}") for i in range(4)]
        w2_loaded = [sem(f"w2_loaded{i}") for i in range(4)]
        pool_step = sem("pool_step")
        consts_ready = sem("consts_ready")
        zeros_ready = sem("zeros_ready")
        wkr_psum, wkr_ready, turn_psum, turn0_ready, turn_ready = (sem("wkr_psum"), sem("wkr_ready"), sem("turn_psum"),
                                                                   sem("turn0_ready"), sem("turn_ready"))
        xT_psum, xT_ready = sem("xT_psum"), sem("xT_ready")
        stats1_ready, mv1_ready, var1_ready, rstd1_ready, xn_ready = (sem("stats1_ready"), sem("mv1_ready"),
                                                                      sem("var1_ready"), sem("rstd1_ready"), sem("xn_ready"))
        z_psum, turns_ready, whole_ready, frac_ready, khat_ready = (sem("z_psum"), sem("turns_ready"), sem("whole_ready"),
                                                                    sem("frac_ready"), sem("khat_ready"))
        v_psum, v_ready, q_psum, q_ready = sem("v_psum"), sem("v_ready"), sem("q_psum"), sem("q_ready")
        tanh_ready, gated_bv_ready, xb_ready = sem("tanh_ready"), sem("gated_bv_ready"), sem("xb_ready")
        scores_psum, max_ready, probs_ready = sem("scores_psum"), sem("max_ready"), sem("probs_ready")
        probsT_psum, probsT_ready, pv_psum = sem("probsT_psum"), sem("probsT_ready"), sem("pv_psum")
        rden_ready, x1_ready = sem("rden_ready"), sem("x1_ready")
        stats2_ready, mv2_ready, var2_ready, rstd2_ready, x2_ready = (sem("stats2_ready"), sem("mv2_ready"),
                                                                      sem("var2_ready"), sem("rstd2_ready"), sem("x2_ready"))
        x2T_psum, x2T_ready, logits_psum = sem("x2T_psum"), sem("x2T_ready"), sem("logits_psum")
        top_ready, top_at_ready, onehot_ready, before_ready = (sem("top_ready"), sem("top_at_ready"), sem("onehot_ready"),
                                                               sem("before_ready"))
        diff_ready, exp_ready, exp_sum_ready = sem("diff_ready"), sem("exp_ready"), sem("exp_sum_ready")
        w_den_ready, w_rec_ready, weight_step, comb_ready = (sem("w_den_ready"), sem("w_rec_ready"), sem("weight_step"),
                                                             sem("comb_ready"))
        neg_mean2_ready, shift2_ready = sem("neg_mean2_ready"), sem("shift2_ready")
        x1_stored, rows_stored, pads_stored = sem("x1_stored"), sem("rows_stored"), sem("pads_stored")
        kept_psum, kept_ready, cum_psum, route_step = sem("kept_psum"), sem("kept_ready"), sem("cum_psum"), sem("route_step")
        pair_ready, warm_ready, exp_top_ready = sem("pair_ready"), sem("warm_ready"), sem("exp_top_ready")
        token_hot_ready = sem("token_hot_ready")
        lane_hot_ready, table_psum = sem("lane_hot_ready"), sem("table_psum")
        gather_at_ready, scatter_at_ready = sem("gather_at_ready"), sem("scatter_at_ready")
        gathered = [sem(f"gathered{e}") for e in range(E)]
        xeT_psum, xeT_ready, up_psum, hid_ready = sem("xeT_psum"), sem("xeT_ready"), sem("up_psum"), sem("hid_ready")
        down_psum, ys_ready, scattered = sem("down_psum"), sem("ys_ready"), sem("scattered")
        weighed_b2_ready = sem("weighed_b2_ready")

        z_bank = [bank[2], bank[3]]
        v_bank = [bank[4], bank[5]]
        xT_bank, q_bank = bank[6], bank[7]
        scores_bank = [bank[0], bank[1]]
        probsT_bank = [bank[2], bank[3]]
        pv_bank, x2T_bank, logits_bank = bank[4], bank[5], [bank[6], bank[7]]
        cum_bank, kept_bank, table_bank = bank[7], bank[4], bank[5]
        warm_bank = bank[1]
        up_bank = [bank[0:2], bank[2:4]]
        xeT_bank = [bank[4], bank[6]]
        down_bank = [bank[5], bank[7]]
        logits_ps = [one[:, 0:TB * E].rearrange("p (h e) -> p h e", h=TB) for one in logits_bank]
        cum_ps = cum_bank[:, 0:T * TOP_K * E]
        kept_ps = kept_bank[:, 0:E]
        table_ps = table_bank[:, 0:SLOT_TILES]

        block = ctx.enter_context(nc.Block())

        @block.sync
        def _(sp):
            def load_rows(dst, src, g, signal):
                sp.dma_start(dst[:, g * GT:(g + 1) * GT, :],
                             src[g * GT * P:(g + 1) * GT * P, :].rearrange("(t p) d -> p t d", p=P)).then_inc(signal[g], 16)

            def store_rows(b0, b1):
                sp.wait_ge(comb_ready, b1)
                sp.wait_ge(x2_ready, b1)
                sp.dma_start(x2_rows[1 + b0 * S:1 + b1 * S, :].rearrange("(t p) d -> p t d", p=P),
                             rows[:, b0 * TB:b1 * TB, :]).then_inc(rows_stored, 16)

            def load_ctx(g):
                cols = slice(g * GT * P, (g + 1) * GT * P)
                sp.dma_start(yT[:, cols], ctxT[:, cols]).then_inc(y_loaded[g], 16)

            sp.dma_start(keys_in[:, :], key_pack).then_inc(keys_loaded, 16)
            for g in range(G):
                if g:
                    load_ctx(g)
                load_rows(x_in, x_rows, g, x_loaded)
            sp.dma_start(b2_all[:, :, :], b2.rearrange("e d -> (e d)").partition_broadcast(P)
                         .rearrange("p (e d) -> p e d", e=E)).then_inc(b2_loaded, 16)
            for i in range(4):
                es = slice(i * E // 4, (i + 1) * E // 4)
                sp.dma_start(w1[:, es, :], W1[es].rearrange("e d h -> d e h")).then_inc(w1_loaded[i], 16)
                for e in range(i * E // 4, (i + 1) * E // 4):
                    sp.dma_start(w2[:, e, :, :], W2[e].rearrange("(c p) d -> p c d", p=P)).then_inc(w2_loaded[i], 16)
            sp.wait_ge(zeros_ready, 1)
            sp.dma_start(x2_rows[0:1, :], zeros[0:1, 0:ROW]).then_inc(pads_stored, 16)
            sp.dma_start(out[0:PAD, :].rearrange("(t p) d -> p t d", p=P),
                         zeros[:, 0:PAD // P * D].rearrange("p (t d) -> p t d", d=D)).then_inc(pads_stored, 16)
            for b in range(B):
                ts = slice(b * TB, (b + 1) * TB)
                sp.wait_ge(x1_ready, b + 1)
                sp.dma_start(out[PAD + b * S:PAD + (b + 1) * S, :].rearrange("(t p) d -> p t d", p=P),
                             x1[:, ts, :]).then_inc(x1_stored, 16)
            for b0, b1 in ROUTE_GROUPS:
                store_rows(b0, b1)
            sp.wait_ge(x1_stored, 16 * B)
            sp.wait_ge(pads_stored, 32)
            sp.wait_ge(scattered, 16 * SLOT_TILES)

        @block.gpsimd
        def _(pool):
            pool.memset(ones[:, :], 1.0).then_inc(warm_ready, 1)
            pool.memset(warm_up[:, :], 1.0).then_inc(warm_ready, 1)
            pool.memset(ident[:, :], 0.0).then_inc(pool_step, 1)
            pool.memset(tri[:, :], 1.0).then_inc(pool_step, 1)
            pool.memset(neg_half[:, :], -0.5).then_inc(consts_ready, 1)
            pool.wait_ge(pool_step, 2)
            pool.affine_select(out=ident[:, :], in_=ident[:, :], compare_op=ALU.not_equal, fill=1.0, base=0,
                               pattern=[[-1, P]], channel_multiplier=1).then_inc(consts_ready, 1)
            pool.affine_select(out=tri[:, :], in_=tri[:, :], compare_op=ALU.is_ge, fill=0.0, base=0,
                               pattern=[[1, P]], channel_multiplier=-1).then_inc(consts_ready, 1)
            pool.memset(before[:, 0, :], 0.0).then_inc(consts_ready, 1)
            small = dict(allow_small_or_imprecise_dtypes=True)
            pool.iota(lane_iota[:, :, :], [[1, P], [0, QUAD]], base=1, channel_multiplier=0,
                      **small).then_inc(consts_ready, 1)
            pool.iota(tile_iota[:, :, :], [[1, SLOT_TILES], [0, QUAD]], base=0, channel_multiplier=0,
                      **small).then_inc(consts_ready, 1)
            pool.iota(expert_iota[:, :], [[1, E]], base=0, channel_multiplier=0, **small).then_inc(consts_ready, 1)
            pool.iota(token_no[:, :, :], [[P, T], [0, TOP_K]], base=1, channel_multiplier=1, **small).then_inc(consts_ready, 1)
            pool.iota(pad_row[:, :].rearrange("p (e s) -> p e s", s=ST), [[0, E], [P, ST]], base=-(PAD - 1),
                      channel_multiplier=1, **small).then_inc(consts_ready, 1)
            pool.memset(zeros[:, :], 0.0).then_inc(zeros_ready, 1)

            def inv_std(mv, rstd, t0, n, var_sem, rstd_sem, k):
                pool.tensor_scalar(rstd[:, t0:t0 + n], mv[:, t0:t0 + n, 1], LN_EPS, None, ALU.add).then_inc(var_sem, 1)
                pool.wait_ge(var_sem, k)
                pool.tensor_tensor(rstd[:, t0:t0 + n], rstd[:, t0:t0 + n], neg_half[:, 0:n], ALU.pow).then_inc(rstd_sem, 1)
                pool.wait_ge(rstd_sem, k)

            def inv_std1(g):
                pool.wait_ge(mv1_ready, g + 1)
                inv_std(mv1, rstd1, g * GT, GT, var1_ready, rstd1_ready, g + 1)

            def fraction(g):
                if g >= 2:
                    pool.wait_ge(khat_ready, g - 1)
                pool.wait_ge(whole_ready, g + 1)
                pool.tensor_tensor(frac[:, g % 2, :], turns[:, g % 2, :], whole[:, g % 2, :],
                                   ALU.subtract).then_inc(frac_ready, 1)

            def add_bv(g):
                pool.wait_ge(xn_ready, g + 1)
                ts = slice(g * GT, (g + 1) * GT)
                pool.tensor_tensor(x_in[:, ts, :], x_in[:, ts, :],
                                   gated_bv[:, :].unsqueeze(1).broadcast_to([P, GT, D]), ALU.add).then_inc(xb_ready, 1)

            inv_std1(0)
            inv_std1(1)
            fraction(0)
            inv_std1(2)
            fraction(1)
            inv_std1(3)
            fraction(2)
            fraction(3)
            pool.wait_ge(tanh_ready, 1)
            pool.wait_ge(bv_loaded, 16)
            pool.tensor_scalar(gated_bv[:, :], bv_all[:, :], tgates[:, 0:1], None, ALU.mult).then_inc(gated_bv_ready, 1)
            pool.wait_ge(gated_bv_ready, 1)
            add_bv(0)

            def norm2(b):
                pool.wait_ge(mv2_ready, b + 1)
                ts = slice(b * TB, (b + 1) * TB)
                pool.tensor_scalar(rstd2[:, ts], mv2[:, ts, 1], LN_EPS, None, ALU.add).then_inc(var2_ready, 1)
                pool.tensor_scalar(neg_mean2[:, ts], mv2[:, ts, 0], -1.0, None, ALU.mult).then_inc(neg_mean2_ready, 1)
                pool.wait_ge(var2_ready, b + 1)
                pool.tensor_tensor(rstd2[:, ts], rstd2[:, ts], neg_half[:, 0:TB], ALU.pow).then_inc(rstd2_ready, 1)
                pool.wait_ge(rstd2_ready, b + 1)
                pool.wait_ge(neg_mean2_ready, b + 1)
                pool.tensor_tensor(shift2[:, ts], neg_mean2[:, ts], rstd2[:, ts], ALU.mult).then_inc(shift2_ready, 1)

            def count(b):
                pool.wait_ge(onehot_ready, b + 1)
                hot = onehot[:, b * TB:(b + 1) * TB, :, :].rearrange("p t k e -> p t (k e)")
                if b:
                    pool.wait_ge(before_ready, b)
                pool.tensor_tensor(pair_sum[:, :], hot[:, 0, :], hot[:, 1, :], ALU.add).then_inc(pair_ready, 1)
                pool.wait_ge(pair_ready, b + 1)
                pool.tensor_tensor(before[:, b + 1, :], before[:, b, :], pair_sum[:, :], ALU.add).then_inc(before_ready, 1)

            def gaps(i):
                b0, b1 = ROUTE_GROUPS[i]
                ts, n = slice(b0 * TB, b1 * TB), (b1 - b0) * TB
                pool.wait_ge(top_ready, b1)
                pool.tensor_tensor(top_diff[:, ts, :], top[:, ts, :], top[:, ts, 0:1].broadcast_to([P, n, 8]),
                                   ALU.subtract).then_inc(diff_ready, 1)

            def weights(i):
                b0, b1 = ROUTE_GROUPS[i]
                ts, n = slice(b0 * TB, b1 * TB), (b1 - b0) * TB
                k = 4 * i
                pool.wait_ge(w_rec_ready, i + 1)
                pool.tensor_tensor(w_top[:, ts, 0], w_den[:, ts], tgates[:, 1:2].broadcast_to([P, n]),
                                   ALU.mult).then_inc(weight_step, 1)
                pool.wait_ge(weight_step, k + 1)
                pool.tensor_tensor(w_top[:, ts, 1], w_top[:, ts, 0], top_exp[:, ts, 1], ALU.mult).then_inc(weight_step, 1)
                pool.tensor_tensor(comb0[:, ts, :], onehot[:, ts, 0, :], w_top[:, ts, 0:1].broadcast_to([P, n, E]),
                                   ALU.mult).then_inc(weight_step, 1)
                pool.wait_ge(weight_step, k + 3)
                pool.tensor_tensor(comb1[:, ts, :], onehot[:, ts, 1, :], w_top[:, ts, 1:2].broadcast_to([P, n, E]),
                                   ALU.mult).then_inc(weight_step, 1)
                pool.wait_ge(weight_step, k + 4)
                pool.tensor_tensor(rows[:, ts, D:ROW], comb0[:, ts, :], comb1[:, ts, :], ALU.add)\
                    .then_inc(comb_ready, b1 - b0)

            for s in range(STEPS):
                if 0 <= s - PV < B:
                    norm2(s - PV)
                if s + 1 < G:
                    add_bv(s + 1)
                if 0 <= s - ROUTE < B - 1:
                    count(s - ROUTE)
                for i, (b0, b1) in enumerate(ROUTE_GROUPS):
                    if s == b1 - 1 + ROUTE:
                        gaps(i)
                    if s == WEIGHT_STEP[i]:
                        weights(i)

            def gather(j):
                pool.indirect_dma_start(out=xe[:, j, :], out_offset=None, in_=x2_rows[:, :],
                                        in_offset=bass.IndirectOffsetOnAxis(ap=gather_at[:, j:j + 1], axis=0))\
                    .then_inc(gathered[j // ST], 16)

            AHEAD = SLOT_TILES // 2 + 1
            GATHERS_AFTER = (2, 2, 2, 1)
            gathers_done = AHEAD
            pool.wait_ge(rows_stored, 16 * len(ROUTE_GROUPS))
            pool.wait_ge(pads_stored, 32)
            pool.wait_ge(gather_at_ready, 1)
            for j in range(AHEAD):
                gather(j)
            pool.wait_ge(scatter_at_ready, 1)
            pool.wait_ge(x1_stored, 16 * B)
            for e in range(E):
                pool.wait_ge(ys_ready, e + 1)
                if e:
                    pool.wait_ge(scattered, 16 * ST * e)
                for j in range(e * ST, (e + 1) * ST):
                    pool.indirect_dma_start(out=out[:, :],
                                            out_offset=bass.IndirectOffsetOnAxis(ap=scatter_at[:, j:j + 1], axis=0),
                                            in_=ys[:, e % 2, j % ST, :], in_offset=None,
                                            compute_op=ALU.add).then_inc(scattered, 16)
                if e < len(GATHERS_AFTER):
                    for j in range(gathers_done, gathers_done + GATHERS_AFTER[e]):
                        gather(j)
                    gathers_done += GATHERS_AFTER[e]
            assert gathers_done == SLOT_TILES

        @block.scalar
        def _(act):
            act.dma_start(yT[:, 0:GT * P], ctxT[:, 0:GT * P]).then_inc(y_loaded[0], 16)
            act.dma_start(gates[:, :], gates_in.partition_broadcast(P)).then_inc(gates_loaded, 16)
            act.dma_start(projs_in[:, :], proj_pack).then_inc(projs_loaded, 16)
            act.dma_start(bv_all[:, :], bv.partition_broadcast(P)).then_inc(bv_loaded, 16)
            act.wait_ge(gates_loaded, 16)
            act.activation(tgates[:, :], gates[:, :], ACT.Tanh).then_inc(tanh_ready, 1)

            def copy_turns(g):
                act.wait_ge(z_psum, g + 1)
                if g >= 2:
                    act.wait_ge(frac_ready, g - 1)
                else:
                    act.wait_ge(turn_ready, 1)
                act.activation(turns[:, g % 2, :], z_bank[g % 2][:, :], ACT.Identity, bias=turn[:, 0:1])\
                    .then_inc(turns_ready, 1)

            def copy_xT(g):
                act.wait_ge(xT_psum, g + 1)
                if g >= 2:
                    act.wait_ge(q_psum, g - 1)
                act.activation(xnT[:, g % 2, :], xT_bank[:, :], ACT.Copy).then_inc(xT_ready, 1)

            def copy_v(g):
                act.wait_ge(v_psum, g + 1)
                act.activation(v[:, g * GT:(g + 1) * GT, :].rearrange("p t d -> p (t d)"), v_bank[g % 2][:, :],
                               ACT.Copy, scale=tgates[:, 0:1]).then_inc(v_ready, 1)

            def cosine(g):
                act.wait_ge(frac_ready, g + 1)
                act.activation(khatT[:, g * GT * P:(g + 1) * GT * P], frac[:, g % 2, :], ACT.Sin,
                               scale=SIN_SCALE).then_inc(khat_ready, 1)

            act.activation(warm_sin[:, :], gates[:, :], ACT.Sin, scale=0.0)
            act.wait_ge(tanh_ready, 1)
            copy_turns(0)
            copy_v(0)
            copy_turns(1)
            copy_v(1)
            copy_xT(0)
            cosine(0)
            copy_turns(2)
            copy_v(2)
            copy_xT(1)
            cosine(1)
            copy_turns(3)
            copy_v(3)
            copy_xT(2)
            cosine(2)
            cosine(3)

            def exps(b):
                act.wait_ge(max_ready, b + 1)
                if b >= 2:
                    act.wait_ge(probsT_psum, b - 1)
                for h in range(TB):
                    act.activation(probs[:, b % 2, h, :], scores_bank[b % 2][:, h * S:(h + 1) * S], ACT.Exp,
                                   bias=neg_max[:, b, h:h + 1], accum_out=den[:, b, h:h + 1]).then_inc(probs_ready, 1)

            def copy_probsT(b):
                act.wait_ge(probsT_psum, b + 1)
                if b >= 2:
                    act.wait_ge(pv_psum, b - 1)
                act.activation(probsT[:, b % 2, :, :].rearrange("p h q -> p (h q)"), probsT_bank[b % 2][:, :],
                               ACT.Copy).then_inc(probsT_ready, 1)

            def copy_x2T(b):
                act.wait_ge(x2T_psum, b + 1)
                if b >= 2:
                    act.wait_ge(logits_psum, b - 1)
                act.activation(x2T[:, b % 2, :], x2T_bank[:, 0:TB * P], ACT.Copy).then_inc(x2T_ready, 1)

            def normalise2(b):
                act.wait_ge(x1_ready, b + 1)
                act.wait_ge(shift2_ready, b + 1)
                for t in range(b * TB, (b + 1) * TB):
                    last = act.activation(rows[:, t, 0:D], x1[:, t, :], ACT.Identity, bias=shift2[:, t:t + 1],
                                          scale=rstd2[:, t:t + 1])
                last.then_inc(x2_ready, 1)

            for s in range(STEPS):
                if s == 1:
                    copy_xT(3)
                for i, (b0, b1) in enumerate(ROUTE_GROUPS):
                    if s == WEIGHT_STEP[i]:
                        ts = slice(b0 * TB, b1 * TB)
                        act.wait_ge(diff_ready, i + 1)
                        act.activation(top_exp[:, ts, :], top_diff[:, ts, :], ACT.Exp).then_inc(exp_ready, 1)
                if 0 <= s - TURN_P < B:
                    copy_probsT(s - TURN_P)
                if s == B:
                    normalise2(B - 1 - NORM2)
                if s < B:
                    exps(s)
                if 0 <= s - TURN_X2 < B:
                    copy_x2T(s - TURN_X2)
                if 0 <= s - NORM2 < B and s != B - 1:
                    normalise2(s - NORM2)

            for e in range(E):
                if e >= 2:
                    act.wait_ge(down_psum, e - 1)
                for c in range(C):
                    act.wait_ge(up_psum, e * (C // 2) + c // 2 + 1)
                    last = act.activation(hid[:, e % 2, c, :],
                                          up_bank[e % 2][c // 2][:, c % 2 * CAPACITY:(c % 2 + 1) * CAPACITY],
                                          ACT.Gelu_apprx_tanh, bias=bias_cols[:, e * C + c:e * C + c + 1])
                    if c % 2:
                        last.then_inc(hid_ready, 1)
                act.wait_ge(gathered[e], 16 * ST)
                if e == 0:
                    act.wait_ge(b2_loaded, 16)
                if e >= 2:
                    act.wait_ge(ys_ready, e - 1)
                for h in range(ST):
                    last = act.activation(weighed_b2[:, e % 2, h, :], b2_all[:, e, :], ACT.Copy,
                                          scale=xe[:, e * ST + h, D + e:D + e + 1])
                last.then_inc(weighed_b2_ready, 1)

        @block.tensor
        def _(pe):
            def turn_x(g):
                if g == 0:
                    pe.wait_ge(consts_ready, CONSTS)
                pe.wait_ge(xn_ready, g + 1)
                if g:
                    pe.wait_ge(xT_ready, g)
                else:
                    pe.wait_ge(wkr_ready, 1)
                for i in range(GT):
                    last = pe.transpose(xT_bank[:, i * P:(i + 1) * P], xn[:, g % 2, i, :], ident[:, :])
                last.then_inc(xT_psum, 1)

            def keys(g):
                pe.wait_ge(y_loaded[g], 16)
                pe.wait_ge(wkr_ready, 1)
                if g >= 2:
                    pe.wait_ge(turns_ready, g - 1)
                pe.matmul(z_bank[g % 2][:, :], wkr[:, :], yT[:, g * GT * P:(g + 1) * GT * P],
                          start=True, stop=True).then_inc(z_psum, 1)
                pe.wait_ge(projs_loaded, 16)
                if g >= 2:
                    pe.wait_ge(v_ready, g - 1)
                for i in range(GT):
                    last = pe.matmul(v_bank[g % 2][:, i * D:(i + 1) * D], yT[:, (g * GT + i) * P:(g * GT + i + 1) * P], wv,
                                     start=True, stop=True)
                last.then_inc(v_psum, 1)

            def queries(g):
                pe.wait_ge(xT_ready, g + 1)
                if g:
                    pe.wait_ge(q_ready, g)
                else:
                    pe.wait_ge(turn0_ready, 1)
                pe.matmul(q_bank[:, :], wq, xnT[:, g % 2, :], start=True, stop=True).then_inc(q_psum, 1)

            def keep_warm(n, cols=512):
                for _ in range(n):
                    pe.matmul(warm_bank[:, 0:cols], ones[:, :], warm_up[:, 0:cols], start=True, stop=True)

            pe.wait_ge(warm_ready, 2)
            keep_warm(5)

            pe.wait_ge(keys_loaded, 16)
            pe.matmul(xT_bank[:, 0:P], wkT, wr, start=True, stop=True).then_inc(wkr_psum, 1)
            pe.matmul(q_bank[:, 0:1], wr, bias_cols[:, BK:BK + 1], start=True, stop=True).then_inc(turn_psum, 1)
            keep_warm(1)

            def scores(b):
                pe.wait_ge(khat_ready, b // GB + 1)
                pe.wait_ge(q_ready, b // GB + 1)
                if b >= 2:
                    pe.wait_ge(probs_ready, TB * (b - 1))
                for h in range(TB):
                    q0 = b * S + h * P
                    last = pe.matmul(scores_bank[b % 2][:, h * S:(h + 1) * S], qT[:, q0:q0 + P],
                                     khatT[:, b * S:(b + 1) * S], start=True, stop=True)
                last.then_inc(scores_psum, 1)

            def turn_probs(b):
                pe.wait_ge(probs_ready, TB * (b + 1))
                if b >= 2:
                    pe.wait_ge(probsT_ready, b - 1)
                for k in range(TB):
                    for h in range(TB):
                        c0 = k * S + h * P
                        last = pe.transpose(probsT_bank[b % 2][:, c0:c0 + P], probs[:, b % 2, h, k * P:(k + 1) * P],
                                            ident[:, :])
                last.then_inc(probsT_psum, 1)

            def weigh_values(b):
                pe.wait_ge(probsT_ready, b + 1)
                pe.wait_ge(v_ready, b // GB + 1)
                if b:
                    pe.wait_ge(x1_ready, b)
                for h in range(TB):
                    for k in range(TB):
                        last = pe.matmul(pv_bank[:, h * D:(h + 1) * D], probsT[:, b % 2, k, h * P:(h + 1) * P],
                                         v[:, b * TB + k, :], start=(k == 0), stop=(k == TB - 1))
                last.then_inc(pv_psum, 1)

            def turn_x2(b):
                pe.wait_ge(x2_ready, b + 1)
                if b:
                    pe.wait_ge(x2T_ready, b)
                for h in range(TB):
                    last = pe.transpose(x2T_bank[:, h * P:(h + 1) * P], rows[:, b * TB + h, 0:D], ident[:, :])
                last.then_inc(x2T_psum, 1)

            def logits(b):
                pe.wait_ge(x2T_ready, b + 1)
                if b >= 2:
                    pe.wait_ge(top_at_ready, b - 1)
                for h in range(TB):
                    last = pe.matmul(logits_ps[b % 2][:, h, :], x2T[:, b % 2, h * P:(h + 1) * P], wg,
                                     start=True, stop=True)
                last.then_inc(logits_psum, 1)

            keys(0)
            keys(1)
            turn_x(0)
            keys(2)
            queries(0)
            turn_x(1)
            keys(3)
            queries(1)
            turn_x(2)
            scores(0)
            queries(2)
            turn_x(3)
            scores(1)

            for s in range(STEPS):
                if s == 2:
                    queries(3)
                if 2 <= s < B:
                    scores(s)
                if 0 <= s - TURN_P < B:
                    turn_probs(s - TURN_P)
                if 0 <= s - PV < B:
                    weigh_values(s - PV)
                if 0 <= s - LOGITS < B:
                    logits(s - LOGITS)
                    if s > B:
                        keep_warm(4, P)
                if 0 <= s - TURN_X2 < B:
                    turn_x2(s - TURN_X2)
                    if s > B:
                        keep_warm(6, P)
            keep_warm(6, P)

            pe.wait_ge(onehot_ready, B)
            by_batch = lambda a: a.rearrange("p (b h c) -> p b h c", b=B, h=TB)
            hot = onehot[:, :, :, :].rearrange("p (b h) k e -> p b h (k e)", h=TB)
            pe.matmul(kept_ps, ones[:, :], hot[:, B - 1, 0, 0:E], start=True, stop=False)
            pe.matmul(kept_ps, ones[:, :], hot[:, B - 1, 1, 0:E], start=False, stop=False)
            pe.wait_ge(before_ready, B - 1)
            pe.matmul(kept_ps, ones[:, :], before[:, B - 1, 0:E], start=False, stop=True).then_inc(kept_psum, 1)
            pe.matmul(cum_ps, tri[:, :], onehot[:, :, :, :].rearrange("p t k e -> p (t k e)"), start=True, stop=False)
            pe.matmul(by_batch(cum_ps), ones[:, :], before[:, 0:B, :].unsqueeze(2).broadcast_to([P, B, TB, TOP_K * E]),
                      start=False, stop=False)
            pe.matmul(by_batch(cum_ps)[:, :, 1, :], ones[:, :], hot[:, :, 0, :], start=False, stop=False)
            pe.wait_ge(kept_ready, 1)
            pe.matmul(cum_ps.rearrange("p (t k e) -> p t k e", t=T, k=TOP_K)[:, :, 1, :], ones[0:1, :],
                      kept[0:1, :].unsqueeze(1).broadcast_to([1, T, E]), start=False, stop=True).then_inc(cum_psum, 1)
            keep_warm(6)
            for n in range(T * TOP_K):
                pe.wait_ge(lane_hot_ready, n + 1)
                if n == 0:
                    pe.wait_ge(token_hot_ready, 1)
                last = pe.matmul(table_ps, lane_hot[:, n // QUAD, :, n % QUAD], token_hot[:, n // QUAD, :, n % QUAD],
                                 start=(n == 0), stop=(n == T * TOP_K - 1))
                if n % (2 * QUAD) == 2 * QUAD - 1 and n < T * TOP_K - 1:
                    keep_warm(1)
            last.then_inc(table_psum, 1)
            keep_warm(17)

            def turn_xe(e):
                pe.wait_ge(gathered[e], 16 * ST)
                if e >= 2:
                    pe.wait_ge(xeT_ready, e - 1)
                for h in range(ST):
                    last = pe.transpose(xeT_bank[e % 2][:, h * P:(h + 1) * P], xe[:, e * ST + h, 0:D], ident[:, :])
                last.then_inc(xeT_psum, 1)

            def up(e):
                if e % 2 == 0:
                    pe.wait_ge(w1_loaded[e // 2], 16)
                pe.wait_ge(xeT_ready, e + 1)
                for c in range(C):
                    if e >= 2 and c % 2 == 0:
                        pe.wait_ge(hid_ready, (e - 2) * (C // 2) + c // 2 + 1)
                    last = pe.matmul(up_bank[e % 2][c // 2][:, c % 2 * CAPACITY:(c % 2 + 1) * CAPACITY],
                                     w1[:, e, c * P:(c + 1) * P], xeT[:, e % 2, :], start=True, stop=True)
                    if c % 2:
                        last.then_inc(up_psum, 1)

            def down(e):
                if e % 2 == 0:
                    pe.wait_ge(w2_loaded[e // 2], 32)
                if e >= 2:
                    pe.wait_ge(ys_ready, e - 1)
                else:
                    pe.wait_ge(scatter_at_ready, 1)
                for half in range(C // 2):
                    pe.wait_ge(hid_ready, e * (C // 2) + half + 1)
                    for h in range(ST):
                        for c in (2 * half, 2 * half + 1):
                            last = pe.matmul(down_bank[e % 2][:, h * D:(h + 1) * D],
                                             hid[:, e % 2, c, h * P:(h + 1) * P], w2[:, e, c, :],
                                             start=(h == 0 and c == 0), stop=(h == ST - 1 and c == C - 1))
                last.then_inc(down_psum, 1)

            turn_xe(0)
            for e in range(E):
                up(e)
                if e + 1 < E:
                    turn_xe(e + 1)
                down(e)

        @block.vector
        def _(dve):
            def stats(src, st, mv, t0, n, st_sem, mv_sem, k):
                for t in range(t0, t0 + n):
                    last = dve.bn_stats(st[:, t, :], src[:, t, :])
                last.then_inc(st_sem, 1)
                dve.wait_ge(st_sem, k)
                for t in range(t0, t0 + n):
                    last = dve.bn_aggr(mv[:, t, :], st[:, t, :])
                last.then_inc(mv_sem, 1)

            def stats_x(g):
                dve.wait_ge(x_loaded[g], 16)
                stats(x_in, stats1, mv1, g * GT, GT, stats1_ready, mv1_ready, g + 1)

            def normalise(g):
                dve.wait_ge(rstd1_ready, g + 1)
                if g >= 2:
                    dve.wait_ge(xT_psum, g - 1)
                for i in range(GT):
                    t = g * GT + i
                    last = dve.tensor_scalar(xn[:, g % 2, i, :], x_in[:, t, :], mv1[:, t, 0:1], rstd1[:, t:t + 1],
                                             ALU.subtract, ALU.mult)
                last.then_inc(xn_ready, 1)

            def round_turns(g):
                dve.wait_ge(turns_ready, g + 1)
                if g >= 2:
                    dve.wait_ge(frac_ready, g - 1)
                dve.tensor_scalar(whole[:, g % 2, :], turns[:, g % 2, :], ROUND_MAGIC, ROUND_MAGIC,
                                  ALU.add, ALU.subtract).then_inc(whole_ready, 1)

            def copy_q(g):
                dve.wait_ge(q_psum, g + 1)
                dve.tensor_scalar(qT[:, g * GT * P:(g + 1) * GT * P], q_bank[:, :], bias_cols[:, BQ:BQ + 1], None,
                                  ALU.add).then_inc(q_ready, 1)

            dve.wait_ge(wkr_psum, 1)
            dve.tensor_scalar(wkr[:, :], xT_bank[:, 0:P], 1.0 / TWO_PI, None, ALU.mult).then_inc(wkr_ready, 1)
            dve.wait_ge(turn_psum, 1)
            dve.tensor_scalar(turn0[:, :], q_bank[:, 0:1], bias_cols[:, BR:BR + 1], None, ALU.add).then_inc(turn0_ready, 1)
            dve.wait_ge(turn0_ready, 1)
            dve.tensor_scalar(turn[:, :], turn0[:, :], 1.0 / TWO_PI, 0.25, ALU.mult, ALU.add).then_inc(turn_ready, 1)

            def scores_max(b):
                dve.wait_ge(scores_psum, b + 1)
                dve.tensor_reduce(neg_max[:, b, :], scores_bank[b % 2][:, :].rearrange("p (h k) -> p h k", h=TB), AX.X,
                                  ALU.max, negate=True).then_inc(max_ready, 1)

            def residual(b):
                dve.wait_ge(rden_ready, b + 1)
                dve.wait_ge(xb_ready, b // GB + 1)
                dve.wait_ge(pv_psum, b + 1)
                for h in range(TB):
                    t = b * TB + h
                    last = dve.scalar_tensor_tensor(out=x1[:, t, :], in0=pv_bank[:, h * D:(h + 1) * D],
                                                    scalar=rden[:, b, h:h + 1], in1=x_in[:, t, :],
                                                    op0=ALU.mult, op1=ALU.add)
                last.then_inc(x1_ready, 1)

            def route_top(b):
                dve.wait_ge(logits_psum, b + 1)
                for h in range(TB):
                    last = dve.max(top[:, b * TB + h, :], logits_ps[b % 2][:, h, :])
                last.then_inc(top_ready, 1)

            def route_at(b):
                dve.wait_ge(top_ready, b + 1)
                for h in range(TB):
                    last = dve.max_index(top_at[:, b * TB + h, :], top[:, b * TB + h, :], logits_ps[b % 2][:, h, :])
                last.then_inc(top_at_ready, 1)

            def route_onehot(b):
                ts = slice(b * TB, (b + 1) * TB)
                dve.wait_ge(top_at_ready, b + 1)
                dve.tensor_tensor(onehot[:, ts, :, :],
                                  expert_iota[:, :].unsqueeze(1).unsqueeze(1).broadcast_to([P, TB, TOP_K, E]),
                                  top_at[:, ts, 0:TOP_K].unsqueeze(3).broadcast_to([P, TB, TOP_K, E]),
                                  ALU.is_equal).then_inc(onehot_ready, 1)

            def weight_sums(i):
                ts = slice(ROUTE_GROUPS[i][0] * TB, ROUTE_GROUPS[i][1] * TB)
                dve.wait_ge(exp_ready, i + 1)
                dve.tensor_reduce(exp_sum[:, ts], top_exp[:, ts, :], AX.X, ALU.add).then_inc(exp_sum_ready, 1)
                dve.tensor_reduce(exp_top[:, ts], top_exp[:, ts, 0:TOP_K], AX.X, ALU.add).then_inc(exp_top_ready, 1)

            def weight_den(i):
                ts = slice(ROUTE_GROUPS[i][0] * TB, ROUTE_GROUPS[i][1] * TB)
                dve.wait_ge(exp_sum_ready, i + 1)
                dve.wait_ge(exp_top_ready, i + 1)
                dve.scalar_tensor_tensor(out=w_den[:, ts], in0=exp_sum[:, ts], scalar=WEIGHT_EPS, in1=exp_top[:, ts],
                                         op0=ALU.mult, op1=ALU.add).then_inc(w_den_ready, 1)

            def weight_recip(i):
                ts = slice(ROUTE_GROUPS[i][0] * TB, ROUTE_GROUPS[i][1] * TB)
                dve.wait_ge(w_den_ready, i + 1)
                dve.reciprocal(w_den[:, ts], w_den[:, ts]).then_inc(w_rec_ready, 1)

            dve.wait_ge(consts_ready, CONSTS)
            stats_x(0)
            stats_x(1)
            normalise(0)
            round_turns(0)
            stats_x(2)
            normalise(1)
            round_turns(1)
            stats_x(3)
            copy_q(0)
            round_turns(2)
            normalise(2)
            round_turns(3)
            copy_q(1)
            normalise(3)
            scores_max(0)
            copy_q(2)
            scores_max(1)

            for s in range(STEPS):
                b, r = s - PV, s - ROUTE
                if s == 2:
                    copy_q(3)
                if 2 <= s < B:
                    scores_max(s)
                if 0 <= b < B:
                    dve.wait_ge(probs_ready, TB * (b + 1))
                    dve.reciprocal(rden[:, b, :], den[:, b, :]).then_inc(rden_ready, 1)
                    residual(b)
                    dve.wait_ge(x1_ready, b + 1)
                    for t in range(b * TB, (b + 1) * TB):
                        last = dve.bn_stats(stats2[:, t, :], x1[:, t, :])
                    last.then_inc(stats2_ready, 1)
                if 0 <= r < B:
                    route_top(r)
                if 0 <= b < B:
                    dve.wait_ge(stats2_ready, b + 1)
                    for t in range(b * TB, (b + 1) * TB):
                        last = dve.bn_aggr(mv2[:, t, :], stats2[:, t, :])
                    last.then_inc(mv2_ready, 1)
                if 0 <= r < B:
                    route_at(r)
                    route_onehot(r)
                for i, (b0, b1) in enumerate(ROUTE_GROUPS[:-1]):
                    if s == WEIGHT_STEP[i]:
                        weight_sums(i)
                        weight_den(i)
                        weight_recip(i)

            step = 0

            def chain(last):
                nonlocal step
                step += 1
                last.then_inc(route_step, 1)
                return step

            n_first = chain(dve.tensor_scalar(first_tile[:, :, :], top_at[:, :, 0:TOP_K], float(ST), None, ALU.mult))
            last_group = len(ROUTE_GROUPS) - 1
            weight_sums(last_group)
            dve.wait_ge(kept_psum, 1)
            dve.tensor_scalar(kept[:, :], kept_ps, float(CAPACITY), None, ALU.min).then_inc(kept_ready, 1)
            weight_den(last_group)
            weight_recip(last_group)
            dve.wait_ge(cum_psum, 1)
            n_picked = chain(dve.tensor_tensor(picked[:, :, :], onehot[:, :, :, :].rearrange("p t k e -> p (t k) e"),
                                               cum_ps.rearrange("p (n e) -> p n e", e=E), ALU.mult))
            dve.wait_ge(route_step, n_picked)
            n_pos = chain(dve.tensor_reduce(pos[:, :], picked[:, :, :], AX.X, ALU.add))
            dve.wait_ge(route_step, n_pos)
            n_upper = chain(dve.tensor_scalar(upper[:, :], pos[:, :], float(P), None, ALU.is_gt))
            n_tile = chain(dve.scalar_tensor_tensor(out=slot_tile[:, :], in0=pos[:, :], scalar=float(P),
                                                    in1=first_tile[:, :, :].rearrange("p t k -> p (t k)"),
                                                    op0=ALU.is_gt, op1=ALU.add))
            dve.wait_ge(route_step, n_upper)
            n_lane = chain(dve.scalar_tensor_tensor(out=lane[:, :], in0=upper[:, :], scalar=-float(P), in1=pos[:, :],
                                                    op0=ALU.mult, op1=ALU.add))
            quads = lambda a, m: (a[:, :].rearrange("p (g q) -> p g q", q=QUAD).unsqueeze(2)
                                  .broadcast_to([P, QUADS, m, QUAD]))
            dve.wait_ge(route_step, n_tile)
            n_hot = chain(dve.tensor_tensor(tile_hot[:, :, :, :],
                                            tile_iota[:, :, :].unsqueeze(1).broadcast_to([P, QUADS, SLOT_TILES, QUAD]),
                                            quads(slot_tile, SLOT_TILES), ALU.is_equal))
            for g in range(0, QUADS, 2):
                if g == 0:
                    dve.wait_ge(route_step, n_lane)
                gs = slice(g, g + 2)
                dve.tensor_tensor(lane_hot[:, gs, :, :], lane_iota[:, :, :].unsqueeze(1).broadcast_to([P, 2, P, QUAD]),
                                  quads(lane, P)[:, gs, :, :], ALU.is_equal).then_inc(lane_hot_ready, 2 * QUAD)
                if g == 0:
                    dve.wait_ge(route_step, n_hot)
                    dve.tensor_tensor(token_hot[:, :, :, :], tile_hot[:, :, :, :],
                                      quads(token_no[:, :, :].rearrange("p t k -> p (t k)"), SLOT_TILES),
                                      ALU.mult).then_inc(token_hot_ready, 1)
            dve.wait_ge(table_psum, 1)
            dve.tensor_copy(gather_at[:, :], table_ps).then_inc(gather_at_ready, 1)
            n_empty = chain(dve.tensor_scalar(empty[:, :], table_ps, 0.0, None, ALU.is_equal))
            dve.wait_ge(route_step, n_empty)
            n_row = chain(dve.tensor_tensor(empty_row[:, :], empty[:, :], pad_row[:, :], ALU.mult))
            dve.wait_ge(route_step, n_row)
            dve.scalar_tensor_tensor(out=scatter_at[:, :], in0=table_ps, scalar=float(PAD - 1), in1=empty_row[:, :],
                                     op0=ALU.add, op1=ALU.add).then_inc(scatter_at_ready, 1)

            def copy_xeT(e):
                dve.wait_ge(xeT_psum, e + 1)
                if e >= 2:
                    dve.wait_ge(up_psum, (e - 1) * (C // 2))
                dve.tensor_copy(xeT[:, e % 2, :], xeT_bank[e % 2][:, 0:CAPACITY]).then_inc(xeT_ready, 1)

            def weigh(e):
                dve.wait_ge(down_psum, e + 1)
                dve.wait_ge(weighed_b2_ready, e + 1)
                if e >= 2:
                    dve.wait_ge(scattered, 16 * ST * (e - 1))
                for h in range(ST):
                    last = dve.scalar_tensor_tensor(out=ys[:, e % 2, h, :], in0=down_bank[e % 2][:, h * D:(h + 1) * D],
                                                    scalar=xe[:, e * ST + h, D + e:D + e + 1],
                                                    in1=weighed_b2[:, e % 2, h, :], op0=ALU.mult, op1=ALU.add)
                last.then_inc(ys_ready, 1)

            copy_xeT(0)
            for e in range(E):
                if e + 1 < E:
                    copy_xeT(e + 1)
                weigh(e)


def _lay_out(inputs):
    col = lambda name: inputs["L0_xattn_" + name][:, None]
    x, ctx = inputs["x"], inputs["ctx_1024"]
    W1, b1 = inputs["L0_ffn_W1"], inputs["L0_ffn_b1"]
    return {
        "x": x,
        "ctxT": ctx.reshape(-1, ctx.shape[-1]).T,
        "gates": np.concatenate([inputs["g_xattn"], inputs["g_ffn"]]),
        "keys": np.concatenate([inputs["L0_xattn_Wk"].T, inputs["L0_xattn_Wr"], b1.reshape(-1, x.shape[-1]).T,
                                col("bq"), col("bk"), col("br")], axis=1),
        "projs": np.concatenate([inputs["L0_xattn_Wv"], inputs["L0_xattn_Wq"], inputs["L0_ffn_Wg"]], axis=1),
        "bv": inputs["L0_xattn_bv"],
        "W1": W1,
        "W2": inputs["L0_ffn_W2"],
        "b2": inputs["L0_ffn_b2"],
    }


def kernel(**inputs):
    import concourse.bacc as _bacc
    from concourse.bass_utils import run_bass_kernel_spmd as _run

    nc = _bacc.Bacc("TRN2", target_bir_lowering=False, num_devices=1)
    inputs = {name: np.asarray(a) for name, a in inputs.items()}
    arrays, args = {}, []
    for name, a in _lay_out(inputs).items():
        a = np.ascontiguousarray(a)
        arrays[f"in_{name}"] = a
        args.append(nc.dram_tensor(f"in_{name}", a.shape, mybir.dt.from_np(a.dtype), kind="ExternalInput").ap())
    B, S, D = inputs["x"].shape
    E = inputs["L0_ffn_W1"].shape[0]
    out = nc.dram_tensor("out", (CAPACITY + B * S, D), F32, kind="ExternalOutput").ap()
    x2_rows = nc.dram_tensor("x2_rows", (1 + B * S, D + E), F32, kind="Internal").ap()
    build(nc, *args, out, x2_rows)
    r = _run(nc, [arrays], core_ids=[0])
    return r.results[0]["out"][CAPACITY:].reshape(B, S, D)
```
